# Optimizing a Trainium2 kernel written in Bass

```python
import numpy as np
import jax
import jax.numpy as jnp

def _softmax(x, axis=-1):
    return jax.nn.softmax(x, axis=axis)

def _gelu(x):
    return jax.nn.gelu(x, approximate=True)

def _silu(x):
    return jax.nn.silu(x)

def _sigmoid(x):
    return jax.nn.sigmoid(x)

def _layernorm(x, axis=-1, eps=1e-05):
    m = jnp.mean(x, axis=axis, keepdims=True)
    v = jnp.var(x, axis=axis, keepdims=True)
    return (x - m) / jnp.sqrt(v + eps)

def _scatter_add(tgt, idx, src, axis=0):
    return tgt.at[idx].add(src)

def _segment_sum(src, seg, n):
    return jax.ops.segment_sum(src, seg, n)
kernel_name = 'mk_adaln_d2_jaxref_r8_4d25de'

def setup_inputs(seed: int=0):
    np.random.seed(seed)
    _w = jnp.asarray

    def _L0_attn_setup():
        import jax, jax.numpy as jnp
        import numpy as np
        DIM = 128
        N_HEADS = 16
        HEAD_DIM = DIM // N_HEADS
        FREQS = [31.0, 37.0, 41.0, 43.0, 47.0]
        TWO_PI = 2.0 * float(np.pi)
        key = jax.random.key(seed)
        ks = jax.random.split(key, 16)
        B, L = (2, 128)
        s = 0.02
        inp = {'x': jax.random.normal(ks[0], (B, L, DIM), dtype=jnp.float32), 'Wq': jax.random.normal(ks[1], (DIM, DIM), dtype=jnp.float32) * s, 'bq': jnp.zeros((DIM,), dtype=jnp.float32), 'Wk': jax.random.normal(ks[2], (DIM, DIM), dtype=jnp.float32) * s, 'bk': jnp.zeros((DIM,), dtype=jnp.float32), 'Wv': jax.random.normal(ks[3], (DIM, DIM), dtype=jnp.float32) * s, 'bv': jnp.zeros((DIM,), dtype=jnp.float32), 'Wo': jax.random.normal(ks[4], (DIM, DIM), dtype=jnp.float32) * s, 'bo': jnp.zeros((DIM,), dtype=jnp.float32), 'alpha': jax.random.normal(ks[5], (N_HEADS, len(FREQS)), dtype=jnp.float32) * 0.1, 'phi': jax.random.uniform(ks[6], (N_HEADS, len(FREQS)), dtype=jnp.float32) * TWO_PI, 'temperature': jnp.ones((1,), dtype=jnp.float32), 'gamma': jnp.ones((DIM,), dtype=jnp.float32), 'beta': jnp.zeros((DIM,), dtype=jnp.float32)}
        return inp
    _L0_attn_in = _L0_attn_setup()

    def _L0_ffn_setup():
        import jax, jax.numpy as jnp
        import numpy as np
        B, S, D, H, E = (8, 256, 128, 512, 16)
        key = jax.random.key(seed)
        ks = jax.random.split(key, 4)
        sd = 1.0 / np.sqrt(D).astype(np.float32)
        sh = 1.0 / np.sqrt(H).astype(np.float32)
        return {'x': jax.random.normal(ks[0], (B, S, D), jnp.float32), 'Wg': jax.random.normal(ks[1], (D, E), jnp.float32) * sd, 'bg': jnp.zeros((E,), jnp.float32), 'W1': jax.random.normal(ks[2], (E, D, H), jnp.float32) * sd, 'b1': jnp.zeros((E, H), jnp.float32), 'W2': jax.random.normal(ks[3], (E, H, D), jnp.float32) * sh, 'b2': jnp.zeros((E, D), jnp.float32)}
    _L0_ffn_in = _L0_ffn_setup()
    _L0_c = _w((lambda *s: np.random.randn(*s).astype(np.float32) * 0.05)(4, 128))
    _L0_wmod = _w((lambda *s: np.random.randn(*s).astype(np.float32) * 0.05)(128, 6 * 128) * 128 ** (-0.5))

    def _L1_attn_setup():
        import jax, jax.numpy as jnp
        import numpy as np
        D_MODEL = 128
        N_HEADS = 16
        D_HEAD = 64
        BATCH = 4
        SEQ = 256
        NEG = -1000000000.0
        key = jax.random.key(seed)
        k1, k2, k3, k4, k5 = jax.random.split(key, 5)
        x = jax.random.normal(k1, (BATCH, SEQ, D_MODEL), dtype=jnp.float32)
        std = 0.02
        wq = jax.random.normal(k2, (N_HEADS, D_HEAD, D_MODEL), dtype=jnp.float32) * std
        wk = jax.random.normal(k3, (N_HEADS, D_HEAD, D_MODEL), dtype=jnp.float32) * std
        wv = jax.random.normal(k4, (N_HEADS, D_HEAD, D_MODEL), dtype=jnp.float32) * std
        wo = jax.random.normal(k5, (D_MODEL, N_HEADS * D_HEAD), dtype=jnp.float32) * std
        return {'x': x, 'wq': wq, 'wk': wk, 'wv': wv, 'wo': wo}
    _L1_attn_in = _L1_attn_setup()

    def _L1_ffn_setup():
        import jax, jax.numpy as jnp
        import numpy as np
        B, S, H, E, I, K = (2, 256, 128, 8, 128, 2)
        ALPHA, LIMIT = (1.702, 7.0)
        key = jax.random.key(seed)
        ks = jax.random.split(key, 5)
        sc = 0.02
        return {'hidden_states': jax.random.normal(ks[0], (B, S, H), jnp.float32), 'router_weight': jax.random.normal(ks[1], (H, E), jnp.float32) * sc, 'gate_up_proj': jax.random.normal(ks[2], (E, H, 2 * I), jnp.float32) * sc, 'gate_up_proj_bias': jnp.zeros((E, 2 * I), jnp.float32), 'down_proj': jax.random.normal(ks[3], (E, I, H), jnp.float32) * sc, 'down_proj_bias': jnp.zeros((E, H), jnp.float32)}
    _L1_ffn_in = _L1_ffn_setup()
    _L1_c = _w((lambda *s: np.random.randn(*s).astype(np.float32) * 0.05)(4, 128))
    _L1_wmod = _w((lambda *s: np.random.randn(*s).astype(np.float32) * 0.05)(128, 6 * 128) * 128 ** (-0.5))
    _d = {'L0_attn_x': _L0_attn_in['x'], 'L0_attn_Wq': _L0_attn_in['Wq'], 'L0_attn_bq': _L0_attn_in['bq'], 'L0_attn_Wk': _L0_attn_in['Wk'], 'L0_attn_bk': _L0_attn_in['bk'], 'L0_attn_Wv': _L0_attn_in['Wv'], 'L0_attn_bv': _L0_attn_in['bv'], 'L0_attn_Wo': _L0_attn_in['Wo'], 'L0_attn_bo': _L0_attn_in['bo'], 'L0_attn_alpha': _L0_attn_in['alpha'], 'L0_attn_phi': _L0_attn_in['phi'], 'L0_attn_temperature': _L0_attn_in['temperature'], 'L0_attn_gamma': _L0_attn_in['gamma'], 'L0_attn_beta': _L0_attn_in['beta'], 'L0_ffn_Wg': _L0_ffn_in['Wg'], 'L0_ffn_bg': _L0_ffn_in['bg'], 'L0_ffn_W1': _L0_ffn_in['W1'], 'L0_ffn_b1': _L0_ffn_in['b1'], 'L0_ffn_W2': _L0_ffn_in['W2'], 'L0_ffn_b2': _L0_ffn_in['b2'], 'L0_c': _L0_c, 'L0_wmod': _L0_wmod, 'L1_attn_wq': _L1_attn_in['wq'], 'L1_attn_wk': _L1_attn_in['wk'], 'L1_attn_wv': _L1_attn_in['wv'], 'L1_attn_wo': _L1_attn_in['wo'], 'L1_ffn_router_weight': _L1_ffn_in['router_weight'], 'L1_ffn_gate_up_proj': _L1_ffn_in['gate_up_proj'], 'L1_ffn_gate_up_proj_bias': _L1_ffn_in['gate_up_proj_bias'], 'L1_ffn_down_proj': _L1_ffn_in['down_proj'], 'L1_ffn_down_proj_bias': _L1_ffn_in['down_proj_bias'], 'L1_c': _L1_c, 'L1_wmod': _L1_wmod}
    _x0 = _d['L0_attn_x']
    _d['L0_attn_x'] = jax.random.normal(jax.random.fold_in(jax.random.key(seed), 1), (4, 1024, 128), dtype=_x0.dtype)
    del _x0
    return _d

def reference(L0_attn_x, L0_attn_Wq, L0_attn_bq, L0_attn_Wk, L0_attn_bk, L0_attn_Wv, L0_attn_bv, L0_attn_Wo, L0_attn_bo, L0_attn_alpha, L0_attn_phi, L0_attn_temperature, L0_attn_gamma, L0_attn_beta, L0_ffn_Wg, L0_ffn_bg, L0_ffn_W1, L0_ffn_b1, L0_ffn_W2, L0_ffn_b2, L0_c, L0_wmod, L1_attn_wq, L1_attn_wk, L1_attn_wv, L1_attn_wo, L1_ffn_router_weight, L1_ffn_gate_up_proj, L1_ffn_gate_up_proj_bias, L1_ffn_down_proj, L1_ffn_down_proj_bias, L1_c, L1_wmod):

    def _L0_attn_ref(x, Wq, bq, Wk, bk, Wv, bv, Wo, bo, alpha, phi, temperature, gamma, beta):
        import jax, jax.numpy as jnp
        import numpy as np
        DIM = 128
        N_HEADS = 16
        HEAD_DIM = DIM // N_HEADS
        FREQS = [31.0, 37.0, 41.0, 43.0, 47.0]
        TWO_PI = 2.0 * float(np.pi)
        B, L, D = x.shape
        H, hd = (N_HEADS, HEAD_DIM)
        q = (x @ Wq.T + bq).reshape(B, L, H, hd).transpose(0, 2, 1, 3)
        k = (x @ Wk.T + bk).reshape(B, L, H, hd).transpose(0, 2, 1, 3)
        v = (x @ Wv.T + bv).reshape(B, L, H, hd).transpose(0, 2, 1, 3)
        sim = jnp.einsum('bhid,bhjd->bhij', q, k) / jnp.sqrt(jnp.asarray(hd, x.dtype))
        temp = jnp.abs(temperature)[0] + 0.1
        sim = sim / temp
        scores = jnp.zeros_like(sim)
        for fi, freq in enumerate(FREQS):
            a = alpha[:, fi][None, :, None, None]
            p = phi[:, fi][None, :, None, None]
            scores = scores + a * jnp.sin(TWO_PI * sim / freq + p)
        w = jax.nn.sigmoid(scores)
        w = w / (jnp.sum(w, axis=-1, keepdims=True) + 1e-10)
        out = jnp.einsum('bhij,bhjd->bhid', w, v)
        out = out.transpose(0, 2, 1, 3).reshape(B, L, D)
        out = out @ Wo.T + bo
        mu = jnp.mean(out, axis=-1, keepdims=True)
        var = jnp.mean(jnp.square(out - mu), axis=-1, keepdims=True)
        return (out - mu) / jnp.sqrt(var + 1e-05) * gamma + beta

    def _L0_ffn_ref(x, Wg, bg, W1, b1, W2, b2):
        import jax, jax.numpy as jnp
        import numpy as np
        B, S, D, H, E = (8, 256, 128, 512, 16)
        d = x.shape[-1]
        xf = x.reshape(-1, d)
        n_tok = xf.shape[0]
        n_exp = Wg.shape[1]
        cap = -(-n_tok // n_exp)
        score = jax.nn.softmax(xf @ Wg + bg, axis=-1)
        gate = jnp.max(score, axis=-1)
        idx = jnp.argmax(score, axis=-1)
        onehot = jax.nn.one_hot(idx, n_exp, dtype=jnp.int32)
        pos = jnp.sum((jnp.cumsum(onehot, axis=0) - 1) * onehot, axis=-1)
        keep = pos < cap
        safe_pos = jnp.where(keep, pos, cap - 1)
        buf = jnp.zeros((n_exp, cap, d), x.dtype).at[idx, safe_pos].add(jnp.where(keep[:, None], xf, 0.0))
        h = jax.nn.relu(jnp.einsum('ecd,edh->ech', buf, W1) + b1[:, None, :])
        y = jnp.einsum('ech,ehd->ecd', h, W2) + b2[:, None, :]
        out = y[idx, safe_pos] * gate[:, None]
        out = jnp.where(keep[:, None], out, 0.0)
        return out.reshape(x.shape)

    def _L1_attn_ref(x, wq, wk, wv, wo):
        import jax, jax.numpy as jnp
        import numpy as np
        D_MODEL = 128
        N_HEADS = 16
        D_HEAD = 64
        BATCH = 4
        SEQ = 256
        NEG = -1000000000.0
        b, s, _ = x.shape
        scale = jnp.sqrt(jnp.asarray(D_HEAD, x.dtype))
        q = jnp.einsum('bsd,hed->bhse', x, wq)
        k = jnp.einsum('bsd,hed->bhse', x, wk)
        v = jnp.einsum('bsd,hed->bhse', x, wv)
        scores = jnp.einsum('bhse,bhte->bhst', q, k) / scale
        causal_mask = jnp.triu(jnp.ones((s, s), dtype=bool), k=1)
        scores = jnp.where(causal_mask, jnp.asarray(NEG, scores.dtype), scores)
        weights = jax.nn.softmax(scores, axis=-1)
        heads = jnp.einsum('bhst,bhte->bhse', weights, v)
        concat = heads.transpose(0, 2, 1, 3).reshape(b, s, N_HEADS * D_HEAD)
        return concat @ wo.T

    def _L1_ffn_ref(hidden_states, router_weight, gate_up_proj, gate_up_proj_bias, down_proj, down_proj_bias):
        import jax, jax.numpy as jnp
        import numpy as np
        B, S, H, E, I, K = (2, 256, 128, 8, 128, 2)
        ALPHA, LIMIT = (1.702, 7.0)
        Bt, St, Ht = hidden_states.shape
        x = hidden_states.reshape(-1, Ht)
        T = x.shape[0]
        logits = x @ router_weight
        top_vals, top_idx = jax.lax.top_k(logits, K)
        scores = jax.nn.softmax(top_vals, axis=-1)
        w = jnp.zeros((T, E), x.dtype).at[jnp.arange(T)[:, None], top_idx].set(scores)
        gu = jnp.einsum('th,ehf->tef', x, gate_up_proj) + gate_up_proj_bias
        gate = gu[..., ::2]
        up = gu[..., 1::2]
        gate = jnp.minimum(gate, LIMIT)
        up = jnp.clip(up, -LIMIT, LIMIT)
        glu = gate * jax.nn.sigmoid(gate * ALPHA)
        act = (up + 1.0) * glu
        down = jnp.einsum('tei,eih->teh', act, down_proj) + down_proj_bias
        out = jnp.einsum('te,teh->th', w, down)
        return out.reshape(Bt, St, Ht)
    x = L0_attn_x
    mod = (_silu(L0_c) @ L0_wmod).reshape(L0_c.shape[0], 6, 1, -1)
    sa, ca, ga, sb, cb, gb = (mod[:, 0], mod[:, 1], mod[:, 2], mod[:, 3], mod[:, 4], mod[:, 5])
    ga = (2 * (ga >= 0) - 1) * jnp.maximum(jnp.abs(ga), 0.25)
    gb = (2 * (gb >= 0) - 1) * jnp.maximum(jnp.abs(gb), 0.25)
    h = _layernorm(x, axis=-1) * (1 + ca) + sa
    x = x + ga * _L0_attn_ref(h, L0_attn_Wq, L0_attn_bq, L0_attn_Wk, L0_attn_bk, L0_attn_Wv, L0_attn_bv, L0_attn_Wo, L0_attn_bo, L0_attn_alpha, L0_attn_phi, L0_attn_temperature, L0_attn_gamma, L0_attn_beta)
    h = _layernorm(x, axis=-1) * (1 + cb) + sb
    x = x + gb * _L0_ffn_ref(h, L0_ffn_Wg, L0_ffn_bg, L0_ffn_W1, L0_ffn_b1, L0_ffn_W2, L0_ffn_b2)
    mod = (_silu(L1_c) @ L1_wmod).reshape(L1_c.shape[0], 6, 1, -1)
    sa, ca, ga, sb, cb, gb = (mod[:, 0], mod[:, 1], mod[:, 2], mod[:, 3], mod[:, 4], mod[:, 5])
    ga = (2 * (ga >= 0) - 1) * jnp.maximum(jnp.abs(ga), 0.25)
    gb = (2 * (gb >= 0) - 1) * jnp.maximum(jnp.abs(gb), 0.25)
    h = _layernorm(x, axis=-1) * (1 + ca) + sa
    x = x + ga * _L1_attn_ref(h, L1_attn_wq, L1_attn_wk, L1_attn_wv, L1_attn_wo)
    h = _layernorm(x, axis=-1) * (1 + cb) + sb
    x = x + gb * _L1_ffn_ref(h, L1_ffn_router_weight, L1_ffn_gate_up_proj, L1_ffn_gate_up_proj_bias, L1_ffn_down_proj, L1_ffn_down_proj_bias)
    return x

_drawn_inputs = setup_inputs


def setup_inputs(seed=0):
    import zlib

    import numpy as np

    out = dict(_drawn_inputs(seed))
    spreads = {'L0_attn_bq': (0.0, 0.8),
     'L0_attn_bk': (0.0, 0.8),
     'L0_attn_bv': (0.0, 0.1),
     'L0_attn_bo': (0.0, 0.1),
     'L0_attn_gamma': (1.0, 0.2),
     'L0_attn_beta': (0.0, 0.35),
     'L0_ffn_bg': (0.0, 0.477),
     'L0_ffn_b1': (0.0, 0.8),
     'L0_ffn_b2': (0.0, 0.8),
     'L1_ffn_gate_up_proj_bias': (0.0, 0.8),
     'L1_ffn_down_proj_bias': (0.0, 0.448)}
    factors = {'L0_attn_Wq': 8.0,
     'L0_attn_Wk': 8.0,
     'L0_attn_Wv': 8.0,
     'L0_attn_alpha': 8.0,
     'L0_attn_phi': 8.0,
     'L1_attn_wq': 8.0,
     'L1_attn_wk': 8.0,
     'L1_attn_wv': 6.391,
     'L1_attn_wo': 6.133,
     'L1_ffn_router_weight': 3.435,
     'L1_ffn_gate_up_proj': 8.0,
     'L1_ffn_down_proj': 8.0,
     'L1_c': 2.831,
     'L1_wmod': 2.753}
    for name, (base, spread) in spreads.items():
        noise = np.random.default_rng([zlib.crc32(name.encode()), seed]).standard_normal(out[name].shape)
        drawn = base * np.exp(spread * noise) if base else spread * noise
        out[name] = jnp.asarray(drawn.astype(out[name].dtype))
    for name, factor in factors.items():
        out[name] = (out[name] * factor).astype(out[name].dtype)
    return out
```

```python
from contextlib import ExitStack

import numpy as np

import concourse.bass as bass
from concourse import mybir

ALU = mybir.AluOpType
ACT = mybir.ActivationFunctionType
AX = mybir.AxisListType
F32 = mybir.dt.float32
F16 = mybir.dt.float16
BF16 = mybir.dt.bfloat16
U32 = mybir.dt.uint32

P = 128
D = 128
B = 4
L = 1024
T = B * L
NT = T // P
TB = L // P
QB = 512
NC = T // QB
H0, HD0 = 16, 8
NF = 5
FREQS = [31.0, 37.0, 41.0, 43.0, 47.0]
NBH = B * H0
QROWS = 3 * HD0
KROWS = 6 * HD0
SROWS = KROWS + 4
MAGIC = 12582912.0
TURN = 6.283185005187988
EPS = 1e-5
E0, CAP, HF = 16, 256, 512
H1, HD1 = 16, 64
HP = H1 // 2
E1, I1 = 8, 128
GALPHA, GLIM = 1.702, 7.0
NEG = -1000000000.0


START = 0


class Ctx:

    def __init__(self, arrays):
        self.src = arrays
        self.sems = []


def sems(nc, g, *names):
    got = [nc.alloc_semaphore(n) for n in names]
    g.sems += got
    return got


def clear_sems(nc, g):
    nc.clear_and_free_semaphores(g.sems)
    nc.all_engine_barrier()
    g.sems = []


def two(nc, g, name):
    return sems(nc, g, name + "_even", name + "_odd")


def stage_mod(nc, g):
    with ExitStack() as ctx:
        c_sb = ctx.enter_context(nc.sbuf_tensor("c_sb", [P, 2, B], F32))
        sc_sb = ctx.enter_context(nc.sbuf_tensor("sc_sb", [P, 2, B], F32))
        wm_sb = ctx.enter_context(nc.sbuf_tensor("wm_sb", [P, 2, 6 * D], F32))
        ps_mod = ctx.enter_context(nc.psum_tensor("ps_mod", [P, 2, 6, B], F32))
        ps_bc = ctx.enter_context(nc.psum_tensor("ps_bc", [P, 6, 4, D], F32))
        gab = ctx.enter_context(nc.sbuf_tensor("gab", [P, 4, 2, 2, B], F32))
        cols = ctx.enter_context(nc.sbuf_tensor("cols", [P, 6, B], F32))
        spread = ctx.enter_context(nc.sbuf_tensor("spread", [P, 6 * B, P], F32))
        small_in, x_in, silu_done, mod_mm, dve, cols_done, spread_done, bc_mm, bc_copied = sems(
            nc, g, "small_in", "x_in", "silu_done", "mod_mm", "mod_dve", "cols_done", "spread_done", "bc_mm", "bc_copied")
        small = [
            (c_sb[:, 0, :], g.src["c0"]), (c_sb[:, 1, :], g.src["c1"]), (wm_sb[:, 0, :], g.src["wm0"]), (wm_sb[:, 1, :], g.src["wm1"]),
            (g.ident[:], g.src["k_ident"]), (g.gamma[:], g.src["gamma_d"]), (g.beta[:], g.src["beta_d"]),
        ]
        block = ctx.enter_context(nc.Block())

        @block.sync
        def _(sp):
            for dst, src in small:
                sp.dma_start(dst, src).then_inc(small_in, 16)
            for k in range(4):
                sp.dma_start(g.x[:, TB * k:TB * (k + 1), :],
                             g.src["x_d"][L * k:L * (k + 1), :].rearrange("(t p) d -> p t d", p=P)).then_inc(x_in, 16)
            sp.wait_ge(x_in, 64)

        @block.scalar
        def _(act):
            act.wait_ge(small_in, 16 * len(small))
            nc.scalar.activation(sc_sb[:], c_sb[:], ACT.Silu).then_inc(silu_done, 1)

        @block.tensor
        def _(pe):
            pe.wait_ge(silu_done, 1)
            for y in range(2):
                for j in range(6):
                    last = nc.tensor.matmul(ps_mod[:, y, j, :], wm_sb[:, y, D * j:D * (j + 1)], sc_sb[:, y, :],
                                            start=True, stop=True)
            last.then_inc(mod_mm, 1)
            pe.wait_ge(spread_done, 6 * B)
            for n in range(6 * B):
                last = nc.tensor.matmul(ps_bc[:, n // 4, n % 4, :], spread[:, n, :], g.ident[:], start=True, stop=True)
            last.then_inc(bc_mm, 1)

        @block.vector
        def _(v):
            v.wait_ge(mod_mm, 1)
            nc.vector.tensor_copy(g.mod[:], ps_mod[:]).then_inc(dve, 1)
            v.wait_ge(dve, 1)
            for y in range(2):
                for j in (1, 4):
                    nc.vector.tensor_scalar(g.mod[:, y, j, :], g.mod[:, y, j, :], 1.0, None, ALU.add).then_inc(dve, 1)
                for k, j in enumerate((2, 5)):
                    nc.vector.tensor_scalar(gab[:, 0, y, k, :], g.mod[:, y, j, :], 0.0, 2.0, ALU.is_ge, ALU.mult).then_inc(dve, 1)
                    nc.vector.scalar_tensor_tensor(out=gab[:, 3, y, k, :], in0=g.mod[:, y, j, :], scalar=-1.0,
                                                   in1=g.mod[:, y, j, :], op0=ALU.mult, op1=ALU.max).then_inc(dve, 1)
            v.wait_ge(dve, 13)
            nc.vector.tensor_scalar(gab[:, 1], gab[:, 3], 0.25, None, ALU.max).then_inc(dve, 1)
            nc.vector.tensor_scalar(gab[:, 2], gab[:, 0], -1.0, None, ALU.add).then_inc(dve, 1)
            v.wait_ge(dve, 15)
            for k, j in enumerate((2, 5)):
                nc.vector.tensor_tensor(g.mod[:, :, j, :], gab[:, 1, :, k, :], gab[:, 2, :, k, :], ALU.mult).then_inc(dve, 1)
            v.wait_ge(dve, 17)
            nc.vector.tensor_scalar(cols[:, 0, :], g.mod[:, 0, 2, :], g.gamma[:, 0:1], None, ALU.mult).then_inc(cols_done, 1)
            nc.vector.tensor_scalar(cols[:, 1, :], g.mod[:, 0, 2, :], g.beta[:, 0:1], None, ALU.mult).then_inc(cols_done, 1)
            for k, (y, j) in enumerate(((0, 4), (0, 3), (0, 5), (1, 5))):
                nc.vector.tensor_copy(cols[:, 2 + k, :], g.mod[:, y, j, :]).then_inc(cols_done, 1)
            v.wait_ge(cols_done, 6)
            nc.vector.memset(g.ones[:], 1.0).then_inc(dve, 1)
            v.wait_ge(dve, 18)
            for n in range(6 * B):
                nc.vector.tensor_scalar(spread[:, n, :], g.ones[:], cols[:, n // B, n % B:n % B + 1], None,
                                        ALU.mult).then_inc(spread_done, 1)
            v.wait_ge(bc_mm, 1)
            nc.vector.tensor_copy(g.bc[:], ps_bc[:]).then_inc(bc_copied, 1)
            v.wait_ge(bc_copied, 1)


def stage_norm(nc, g, y, j, token_major):
    scale, shift = j + 1, j
    with ExitStack() as ctx:
        st = ctx.enter_context(nc.sbuf_tensor(f"st{y}{j}", [P, NT, 6], F32))
        mv = ctx.enter_context(nc.sbuf_tensor(f"mv{y}{j}", [P, NT, 2], F32))
        sd = ctx.enter_context(nc.sbuf_tensor(f"sd{y}{j}", [P, 3, NT], F32))
        psT = ctx.enter_context(nc.psum_tensor(f"psT{y}{j}", [P, NC, QB], F32))
        h = g.h
        stats, aggr, veps, root, rinv, hn, hmod, turned, moved = sems(
            nc, g, *[f"n{y}{j}_{s}" for s in ("stats", "aggr", "veps", "root", "rinv", "hn", "hmod", "turned", "moved")])
        block = ctx.enter_context(nc.Block())

        @block.vector
        def _(v):
            for t in range(NT):
                nc.vector.bn_stats(st[:, t, :], g.x[:, t, :]).then_inc(stats, 1)
            for t in range(NT):
                v.wait_ge(stats, t + 1)
                nc.vector.bn_aggr(mv[:, t, :], st[:, t, :]).then_inc(aggr, 1)
            v.wait_ge(aggr, NT)
            nc.vector.tensor_scalar(sd[:, 0, :], mv[:, :, 1], EPS, None, ALU.add).then_inc(veps, 1)
            v.wait_ge(root, 1)
            nc.vector.reciprocal(sd[:, 2, :], sd[:, 1, :]).then_inc(rinv, 1)
            v.wait_ge(rinv, 1)
            for t in range(NT):
                nc.vector.tensor_scalar(h[:, t, :], g.x[:, t, :], mv[:, t, 0:1], sd[:, 2, t:t + 1],
                                        ALU.subtract, ALU.mult).then_inc(hn, 1)
                if token_major and t % TB == TB - 1:
                    b = t // TB
                    hb = h[:, TB * b:TB * (b + 1), :]
                    v.wait_ge(hn, t + 1)
                    nc.vector.tensor_tensor(hb, hb, g.bc[:, 2, b:b + 1, :].to_broadcast([P, TB, D]),
                                            ALU.mult).then_inc(hmod, 1)
                    v.wait_ge(hmod, 2 * b + 1)
                    nc.vector.tensor_tensor(hb, hb, g.bc[:, 3, b:b + 1, :].to_broadcast([P, TB, D]),
                                            ALU.add).then_inc(hmod, 1)

        @block.scalar
        def _(act):
            act.wait_ge(veps, 1)
            nc.scalar.activation(sd[:, 1, :], sd[:, 0, :], ACT.Sqrt).then_inc(root, 1)
            for c in range(NC):
                b = c * QB // L
                act.wait_ge(turned, c + 1)
                if token_major:
                    nc.scalar.activation(g.hT[:, c * QB:(c + 1) * QB], psT[:, c, :], ACT.Copy).then_inc(moved, 1)
                else:
                    nc.scalar.activation(g.hT[:, c * QB:(c + 1) * QB], psT[:, c, :], ACT.Identity,
                                         bias=g.mod[:, y, shift, b:b + 1],
                                         scale=g.mod[:, y, scale, b:b + 1]).then_inc(moved, 1)
            act.wait_ge(moved, NC)

        @block.tensor
        def _(pe):
            for c in range(NC):
                if token_major:
                    pe.wait_ge(hmod, 2 * (c * QB // L) + 2)
                else:
                    pe.wait_ge(hn, 4 * c + 4)
                for k in range(4):
                    last = nc.tensor.transpose(psT[:, c, P * k:P * (k + 1)], h[:, 4 * c + k, :], g.ident[:])
                last.then_inc(turned, 1)


def stage_qkv0(nc, g):
    with ExitStack() as ctx:
        def sb(n, s, dt=F32):
            return ctx.enter_context(nc.sbuf_tensor(n, s, dt))
        wq, wk, wv, cb, bvr = sb("wq", [P, D]), sb("wk", [P, D]), sb("wv", [P, D]), sb("cb", [P, 8]), sb("bvr", [1, D])
        ph = sb("ph", [NF * H0, 8])
        pb = sb("pb", [NF * H0, 4], BF16)
        phr = sb("phr", [NF * H0, 4, L], BF16)
        one80 = sb("one80", [NF * H0, L])
        q_sb, k_sb = sb("q_sb", [P, 2, QB]), sb("k_sb", [P, 2, QB])
        res = sb("res", [P, 2, QB])
        qp = sb("qp", [P, 2, 3, QB], BF16)
        kp = sb("kp", [P, 2, 3, QB], BF16)
        psq = ctx.enter_context(nc.psum_tensor("psq", [P, 2, QB], F32))
        psk = ctx.enter_context(nc.psum_tensor("psk", [P, 2, QB], F32))
        psv = ctx.enter_context(nc.psum_tensor("psv", [P, 2, 4, D], F32))
        pss = ctx.enter_context(nc.psum_tensor("pss", [P, B], F32))
        (w_in, scale_d, phase_d, ph_out, q_mm, k_mm, v_mm, q_copied, k_copied, v_copied, hi_d, res_d, mid_d, lo_d,
         khi_d, kmid_d, klo_d, s_mm, s_copied, vset) = sems(
            nc, g, "w_in", "scale_d", "phase_d", "ph_out", "q_mm", "k_mm", "v_mm", "q_copied", "k_copied", "v_copied",
            "hi_d", "res_d", "mid_d", "lo_d", "khi_d", "kmid_d", "klo_d", "s_mm", "s_copied", "vset")
        q_out, k_out = two(nc, g, "q_out"), two(nc, g, "k_out")
        loads = [(wq[:], g.src["wq0"]), (wk[:], g.src["wk0"]), (wv[:], g.src["wv0"]), (cb[:, 0:1], g.src["bq0"]), (cb[:, 1:2], g.src["bk0"]), (bvr[:], g.src["bv0"]),
                 (cb[:, 2:3], g.src["temp"].to_broadcast([P, 1])), (ph[:, 0:1], g.src["phi"]),
                 (g.alpha[:], g.src["alpha_d"].to_broadcast([P, NBH * NF]))]
        block = ctx.enter_context(nc.Block())

        @block.sync
        def _(sp):
            for dst, src in loads:
                sp.dma_start(dst, src).then_inc(w_in, 16)
            sp.wait_ge(phase_d, 10)
            for b in range(B):
                sp.dma_start(g.PH[H0 * b:H0 * (b + 1)].rearrange("h f r n -> (h f) r n"), phr[:]).then_inc(ph_out, 16)
            for c in range(NC):
                b, col = c * QB // L, c * QB % L
                sp.wait_ge(klo_d, c + 1)
                for row, part in enumerate((0, 0, 0, 1, 1, 2)):
                    sp.dma_start(g.KS[H0 * b:H0 * (b + 1), row, :, col:col + QB],
                                 kp[:, c % 2, part, :]).then_inc(k_out[c % 2], 16)
                for f in range(NF):
                    m = c * NF + f
                    sp.wait_ge(lo_d, m + 1)
                    for part in range(3):
                        sp.dma_start(g.QS[H0 * b:H0 * (b + 1), part, :, f, col:col + QB],
                                     qp[:, m % 2, part, :]).then_inc(q_out[m % 2], 16)
            sp.wait_ge(ph_out, 16 * B)
            for k in range(2):
                sp.wait_ge(k_out[k], 16 * 6 * NC // 2)
                sp.wait_ge(q_out[k], 16 * 3 * NF * NC // 2)

        @block.tensor
        def _(pe):
            pe.wait_ge(w_in, 16 * len(loads))
            for c in range(NC):
                hc = g.hT[:, c * QB:(c + 1) * QB]
                if c >= 2:
                    pe.wait_ge(q_copied, c - 1)
                nc.tensor.matmul(psq[:, c % 2, :], wq[:], hc, start=True, stop=True).then_inc(q_mm, 1)
                if c >= 2:
                    pe.wait_ge(k_copied, c - 1)
                nc.tensor.matmul(psk[:, c % 2, :], wk[:], hc, start=True, stop=True).then_inc(k_mm, 1)
                if c >= 2:
                    pe.wait_ge(v_copied, c - 1)
                for k in range(4):
                    nc.tensor.matmul(psv[:, c % 2, k, :], hc[:, P * k:P * (k + 1)], wv[:], start=True, stop=False)
                    last = nc.tensor.matmul(psv[:, c % 2, k, :], g.ones[0:1, :], bvr[:], start=False, stop=True)
                last.then_inc(v_mm, 1)
            pe.wait_ge(v_copied, NC)
            pe.wait_ge(vset, 1)
            for b in range(B):
                for t in range(TB):
                    last = nc.tensor.matmul(pss[:, b:b + 1], g.vtok[:, TB * b + t, :], g.ones[:, 0:1],
                                            start=(t == 0), stop=(t == TB - 1))
            last.then_inc(s_mm, 1)

        @block.scalar
        def _(act):
            act.wait_ge(scale_d, 4)
            for c in range(NC):
                act.wait_ge(v_mm, c + 1)
                nc.scalar.activation(g.vtok[:, 4 * c:4 * c + 4, :], psv[:, c % 2, :, :], ACT.Copy).then_inc(v_copied, 1)
                act.wait_ge(k_copied, c + 1)
                if c >= 2:
                    act.wait_ge(k_out[c % 2], 16 * 6 * (c // 2))
                nc.scalar.activation(kp[:, c % 2, 0, :], k_sb[:, c % 2, :], ACT.Copy).then_inc(khi_d, 1)
                for f in range(NF):
                    m = c * NF + f
                    act.wait_ge(q_copied, c + 1)
                    if m >= 2:
                        act.wait_ge(q_out[m % 2], 16 * 3 * (m // 2))
                    nc.scalar.activation(qp[:, m % 2, 0, :], q_sb[:, c % 2, :], ACT.Copy, scale=1.0 / FREQS[f]).then_inc(hi_d, 1)
                    act.wait_ge(res_d, c + m + 2)
                    nc.scalar.activation(qp[:, m % 2, 1, :], res[:, (c + m + 1) % 2, :], ACT.Copy).then_inc(mid_d, 1)

        @block.vector
        def _(v):
            v.wait_ge(w_in, 16 * len(loads))
            nc.vector.scalar_tensor_tensor(out=cb[:, 3:4], in0=cb[:, 2:3], scalar=-1.0, in1=cb[:, 2:3], op0=ALU.mult,
                                           op1=ALU.max).then_inc(scale_d, 1)
            v.wait_ge(scale_d, 1)
            nc.vector.tensor_scalar(cb[:, 4:5], cb[:, 3:4], 0.1, float(np.sqrt(HD0)), ALU.add, ALU.mult).then_inc(scale_d, 1)
            v.wait_ge(scale_d, 2)
            nc.vector.reciprocal(cb[:, 5:6], cb[:, 4:5]).then_inc(scale_d, 1)
            v.wait_ge(scale_d, 3)
            steps = [
                lambda: nc.vector.tensor_scalar(ph[:, 1:2], ph[:, 0:1], float(1 / (2 * np.pi)), None, ALU.mult),
                lambda: nc.vector.tensor_scalar(ph[:, 2:3], ph[:, 1:2], MAGIC, -MAGIC, ALU.add, ALU.add),
                lambda: nc.vector.tensor_tensor(ph[:, 3:4], ph[:, 1:2], ph[:, 2:3], ALU.subtract),
                lambda: nc.vector.tensor_copy(pb[:, 0:1], ph[:, 3:4]),
                lambda: nc.vector.tensor_tensor(ph[:, 4:5], ph[:, 3:4], pb[:, 0:1], ALU.subtract),
                lambda: nc.vector.tensor_copy(pb[:, 1:2], ph[:, 4:5]),
                lambda: nc.vector.tensor_tensor(ph[:, 5:6], ph[:, 4:5], pb[:, 1:2], ALU.subtract),
            ]
            nc.vector.memset(one80[:], 1.0).then_inc(scale_d, 1)
            for n, step in enumerate(steps):
                step().then_inc(phase_d, 1)
                v.wait_ge(phase_d, n + 1)
            v.wait_ge(scale_d, 4)
            for r, src in enumerate((ph[:, 3:4], ph[:, 4:5], ph[:, 5:6])):
                ins = nc.vector.tensor_scalar(phr[:, r, :], one80[:], src, None, ALU.mult)
                if r < 2:
                    ins.then_inc(phase_d, 1)
            nc.vector.memset(phr[:, 3, :], 0.0).then_inc(phase_d, 1)
            for c in range(NC):
                v.wait_ge(q_mm, c + 1)
                if c >= 2:
                    v.wait_ge(hi_d, NF * (c - 1))
                nc.vector.tensor_scalar(q_sb[:, c % 2, :], psq[:, c % 2, :], cb[:, 0:1], cb[:, 5:6],
                                        ALU.add, ALU.mult).then_inc(q_copied, 1)
                v.wait_ge(k_mm, c + 1)
                if c >= 2:
                    v.wait_ge(khi_d, c - 1)
                nc.vector.tensor_scalar(k_sb[:, c % 2, :], psk[:, c % 2, :], cb[:, 1:2], None, ALU.add).then_inc(k_copied, 1)
                v.wait_ge(khi_d, c + 1)
                if c + c * NF >= 2:
                    v.wait_ge(mid_d, c * NF - 1)
                nc.vector.tensor_tensor(res[:, (c + c * NF) % 2, :], k_sb[:, c % 2, :], kp[:, c % 2, 0, :],
                                        ALU.subtract).then_inc(res_d, 1)
                v.wait_ge(res_d, c + c * NF + 1)
                nc.vector.tensor_copy(kp[:, c % 2, 1, :], res[:, (c + c * NF) % 2, :]).then_inc(kmid_d, 1)
                v.wait_ge(kmid_d, c + 1)
                nc.vector.tensor_tensor(kp[:, c % 2, 2, :], res[:, (c + c * NF) % 2, :], kp[:, c % 2, 1, :],
                                        ALU.subtract).then_inc(klo_d, 1)
                for f in range(NF):
                    m = c * NF + f
                    r = (c + m + 1) % 2
                    v.wait_ge(hi_d, m + 1)
                    nc.vector.scalar_tensor_tensor(out=res[:, r, :], in0=q_sb[:, c % 2, :], scalar=1.0 / FREQS[f],
                                                   in1=qp[:, m % 2, 0, :], op0=ALU.mult, op1=ALU.subtract).then_inc(res_d, 1)
                    v.wait_ge(mid_d, m + 1)
                    nc.vector.tensor_tensor(qp[:, m % 2, 2, :], res[:, r, :], qp[:, m % 2, 1, :], ALU.subtract).then_inc(lo_d, 1)
            v.wait_ge(s_mm, 1)
            nc.vector.tensor_copy(g.vsum[:], pss[:]).then_inc(s_copied, 1)
            v.wait_ge(s_copied, 1)

        @block.gpsimd
        def _(pool):
            nc.gpsimd.memset(g.v9[:], 1.0).then_inc(vset, 1)
            pool.wait_ge(vset, 1)
            pool.wait_ge(v_copied, NC)
            for b in range(B):
                last = nc.gpsimd.tensor_copy(g.v9[:, H0 * b:H0 * (b + 1), :, 0:HD0].rearrange("p h t d -> p t h d"),
                                             g.vtok[:, TB * b:TB * (b + 1), :].rearrange("p t (h d) -> p t h d", h=H0))
            last.then_inc(vset, 1)
            pool.wait_ge(vset, 2)


V0, P1, P3, V2, P4 = range(5)
SIN_ORDER = [P1, V0, P3, P4, V2]
SLOTS = 3
UNITS = 8
BODY = 2


def slot_plan():
    steps = [(u, s) for u in range(UNITS * BODY) for s in range(NF)]
    total = NF * UNITS * BODY
    read = [k - SLOTS for k in range(SLOTS)]
    slot, after = {}, {}
    for u, s in steps:
        slot[(u, s)] = k = read.index(min(read))
        read[k] = NF * u + SIN_ORDER.index(s)
    read = [q - total for q in read]
    for u, s in steps:
        k = slot[(u, s)]
        after[(u, s)], read[k] = read[k], NF * u + SIN_ORDER.index(s)
    return slot, after


def stage_scores0(nc, g):
    SC, AC, TC, VC, OC = 5, 42, 3, 12, 1
    slot, after = slot_plan()
    with ExitStack() as ctx:
        def sb(n, s, dt=F32):
            return ctx.enter_context(nc.sbuf_tensor(n, s, dt))
        qst = sb("qst", [P, 2, NF, L], BF16)
        kst = sb("kst", [P, 2, L], BF16)
        kneg = sb("kneg", [P, 2, L], BF16)
        nil = sb("nil", [P, L], BF16)
        mrow = sb("mrow", [P, QB], BF16)
        negi = sb("negi", [P, P], F16)
        vcur = sb("vcur", [P, 2, TB, 32])
        acur = sb("acur", [P, 2, NF])
        turns = sb("turns", [P, 2, 2, QB], F16)
        wave = sb("wave", [P, NF, 2, QB])
        acc = sb("acc", [P, 2, 2, QB])
        wt = sb("wt", [P, 2, 2, QB])
        obuf = sb("obuf", [P, 2, QB])
        credit = sb("credit", [P, 10])
        ps = ctx.enter_context(nc.psum_tensor("ps_steps", [P, SLOTS, 2, QB], F32))
        pv = ctx.enter_context(nc.psum_tensor("ps_pv", [P, QB], F32))
        (cleared, stack_used, kneg_ready, v_ready, alpha_ready, raw_ready, turns_ready, angle_ready,
         sines, sums, tanhs, products, evacs, pv_cleared, mrow_in, silu_loaded) = sems(
            nc, g, "cleared", "stack_used", "kneg_ready", "v_ready", "alpha_ready", "raw_ready",
            "turns_ready", "angle_ready", "sines", "sums", "tanhs", "products", "evacs", "pv_cleared", "mrow_in", "silu_loaded")
        stack_in, stored = two(nc, g, "stack_in"), two(nc, g, "stored")
        CLEAR = 12
        block = ctx.enter_context(nc.Block())
        NLOAD = 5

        @block.sync
        def _(sp):
            sp.dma_start(mrow[:], g.src["k_mrow"]).then_inc(mrow_in, 16)
            sp.wait_ge(cleared, CLEAR)
            with sp.Fori(0, NBH // BODY) as i:
                for w in range(BODY):
                    n = i * BODY + w
                    sp.wait_ge(stack_used, n + 1)
                    for lo, k in ((0, 3), (3 * HD0, 2), (5 * HD0, 1)):
                        sp.dma_start(qst[lo:lo + k * HD0, w, :, :],
                                     g.QS[n, 0:k].rearrange("k d f n -> (k d) f n")).then_inc(stack_in[w], 16)
                    sp.dma_start(qst[KROWS:SROWS, w, :, :], g.PH[n].rearrange("f r n -> r f n")).then_inc(stack_in[w], 16)
                    sp.dma_start(kst[0:KROWS, w, :], g.KS[n].rearrange("k d n -> (k d) n")).then_inc(stack_in[w], 16)

        @block.gpsimd
        def _(pool):
            pool.memset(kst[:], 1.0).then_inc(cleared, 1)
            pool.memset(kneg[:], 1.0).then_inc(cleared, 1)
            pool.memset(qst[:], 0.0).then_inc(cleared, 1)
            pool.memset(vcur[:], 0.0).then_inc(cleared, 1)
            pool.memset(acur[:], 0.0).then_inc(cleared, 1)
            pool.memset(nil[:], 0.0).then_inc(cleared, 1)
            pool.wait_ge(cleared, CLEAR)
            with pool.Fori(0, NBH // BODY) as i:
                for w in range(BODY):
                    n = i * BODY + w
                    pool.wait_ge(products, n * UNITS + (VC - 9))
                    nc.gpsimd.tensor_copy(vcur[:, w, :, 0:HD0 + 1], g.v9[:, bass.ds(n, 1), :, :].rearrange(
                        "p o t d -> p (o t) d")).then_inc(v_ready, 1)
                    pool.wait_ge(sums, n * (5 * UNITS) + (AC - 41))
                    nc.gpsimd.tensor_copy(acur[:, w, :], g.alpha[:, bass.ds(n * NF, NF)]).then_inc(alpha_ready, 1)
                    pool.wait_ge(stack_in[w], i * (16 * NLOAD) + 16 * NLOAD)
                    nc.gpsimd.tensor_tensor(kneg[:, w, :], nil[:], kst[:, w, :], ALU.subtract).then_inc(kneg_ready, 1)

        def pv_product(pe, prev_w, uu, U, n_prev, head_done=False):
            jp, qh = uu % UNITS // 2, uu % 2
            pe.wait_ge(tanhs, U + (TC - 1))
            if jp == 0:
                pe.wait_ge(evacs, n_prev + OC)
                if qh == 0:
                    pe.wait_ge(v_ready, n_prev + 1)
            for a in range(2):
                r = 32 * (2 * qh + a)
                last = nc.tensor.matmul(pv[r:r + 32, :], vcur[:, prev_w, 2 * jp + a, :], wt[:, uu % 2, a, :],
                                        start=(jp == 0), stop=(jp == 3), skip_group_check=True)
                if a == 0 and head_done:
                    last.then_inc(stack_used, 1)
            last.then_inc(products, 1)

        @block.tensor
        def _(pe):
            pe.wait_ge(cleared, CLEAR)
            pe.wait_ge(mrow_in, 16)
            for r in range(0, P, 32):
                last = nc.tensor.matmul(pv[r:r + 32, :], vcur[:, BODY - 1, 0, :], wt[:, 1, 0, :], start=True, stop=True,
                                        skip_group_check=True)
            last.then_inc(pv_cleared, 1)

            def angles(w, uu, s, neg, mag, start):
                jp, qh = uu % UNITS // 2, uu % 2
                for a in range(2):
                    j = 2 * jp + a
                    k = (kneg if neg else kst)[:, w, P * j:P * (j + 1)]
                    q = mrow[:] if mag else qst[:, w, s, QB * qh:QB * (qh + 1)]
                    last = nc.tensor.matmul(ps[:, slot[(uu, s)], a, :], k, q, start=start,
                                            stop=not neg and not mag, skip_group_check=True)
                return last

            def less_turns(uu, s, k):
                for a in range(2):
                    last = nc.tensor.matmul(ps[:, slot[(uu, s)], a, :], negi[:], turns[:, k, a, :], start=False,
                                            stop=True, skip_group_check=True)
                return last

            with pe.Fori(0, NBH // BODY) as i:
                for uu in range(UNITS * BODY):
                    w, n, U = uu // UNITS, i * BODY + uu // UNITS, i * (UNITS * BODY) + uu
                    if uu % UNITS == 0:
                        pe.wait_ge(stack_in[w], i * (16 * NLOAD) + 16 * NLOAD)
                        pe.wait_ge(kneg_ready, n + 1)

                    def slot_free(s):
                        pe.wait_ge(sines, i * (5 * UNITS * BODY) + (after[(uu, s)] + 1 + SC))

                    def magic_step(s):
                        slot_free(s)
                        angles(w, uu, s, True, True, True)
                        angles(w, uu, s, True, False, False)
                        angles(w, uu, s, False, True, False)
                        angles(w, uu, s, False, False, False).then_inc(angle_ready, 1)

                    slot_free(V0)
                    angles(w, uu, V0, False, False, True).then_inc(raw_ready, 1)
                    magic_step(P1)
                    pe.wait_ge(turns_ready, U * 2 + 1)
                    less_turns(uu, V0, 0).then_inc(angle_ready, 1)
                    magic_step(P3)
                    slot_free(V2)
                    angles(w, uu, V2, False, False, True).then_inc(raw_ready, 1)
                    magic_step(P4)
                    pe.wait_ge(turns_ready, U * 2 + 2)
                    less_turns(uu, V2, 1).then_inc(angle_ready, 1)
                    prev = (uu - 1) % (UNITS * BODY)
                    n_prev = i * BODY + (-1 if uu == 0 else (uu - 1) // UNITS)
                    pv_product(pe, prev // UNITS, prev, U, n_prev, uu % UNITS == UNITS - 1)
            last_u = UNITS * BODY - 1
            pv_product(pe, BODY - 1, last_u, NBH * UNITS, NBH - 1)

        @block.scalar
        def _(act):
            act.wait_ge(cleared, CLEAR)

            def tanh(uu, U):
                act.wait_ge(sums, U * 5 + (AC - 1))
                act.wait_ge(products, U + (VC - 3))
                nc.scalar.activation(wt[:, uu % 2, :, :], acc[:, uu % 2, :, :], ACT.Tanh, scale=0.5).then_inc(tanhs, 1)

            def store(w, n):
                act.wait_ge(evacs, n + 1)
                for k in range(4):
                    act.dma_start(g.NUM[n, k], obuf[32 * k:32 * k + HD0 + 1, w, :]).then_inc(stored[w], 16)

            nc.scalar.activation(credit[:, 8:9], credit[:, 9:10], ACT.Silu).then_inc(silu_loaded, 1)
            with act.Fori(0, NBH // BODY) as i:
                for uu in range(UNITS * BODY):
                    U = i * (UNITS * BODY) + uu
                    for a, s in enumerate(SIN_ORDER):
                        act.wait_ge(angle_ready, U * 5 + (a + 1))
                        act.wait_ge(sums, U * 5 + (a - 5 + AC))
                        nc.scalar.activation(wave[:, a, :, :], ps[:, slot[(uu, s)], :, :], ACT.Sin,
                                             scale=TURN).then_inc(sines, 1)
                        if a == 1:
                            tanh((uu - 1) % 2, U)
                    if uu % UNITS == 3:
                        store((uu // UNITS - 1) % BODY, i * BODY + uu // UNITS)
            tanh(1, NBH * UNITS)
            store(BODY - 1, NBH)
            act.wait_ge(stored[0], 16 + 64 * (NBH // 2))
            act.wait_ge(stored[1], 16 + 64 * (NBH // 2 + 1))

        @block.vector
        def _(v):
            v.memset(turns[:], 0.0).then_inc(cleared, 1)
            v.memset(credit[:, 9:10], 0.0).then_inc(cleared, 1)
            v.memset(wave[:], 0.0).then_inc(cleared, 1)
            v.memset(acc[:], 0.0).then_inc(cleared, 1)
            v.memset(wt[:], 0.0).then_inc(cleared, 1)
            nc.vector.tensor_scalar(negi[:], g.ident[:], -1.0, None, ALU.mult).then_inc(cleared, 1)
            for k, (done, count) in enumerate(((stack_used, BODY), (sines, SC), (sums, AC - 4), (tanhs, TC - 2),
                                               (products, VC - 2), (stored[0], 16), (stored[1], 16))):
                v.memset(credit[:, k:k + 1], 0.0).then_inc(done, count)
            v.wait_ge(cleared, CLEAR)
            v.wait_ge(pv_cleared, 1)

            def whole_turns(uu, s, U, k):
                v.wait_ge(raw_ready, U * 2 + (k + 1))
                nc.vector.tensor_scalar(turns[:, k, :, :], ps[:, slot[(uu, s)], :, :], MAGIC, -MAGIC, ALU.add,
                                        ALU.add).then_inc(turns_ready, 1)

            def add_wave(uu, a, U):
                w, s = uu // UNITS, SIN_ORDER[a]
                v.wait_ge(sines, U * 5 + (a + 1 + SC))
                v.wait_ge(sums, U * 5 + (a + AC - 1))
                src, dst = wave[:, a, :, :], acc[:, uu % 2, :, :]
                if a == 0:
                    v.wait_ge(tanhs, U + (TC - 2))
                    nc.vector.tensor_scalar(dst, src, acur[:, w, s:s + 1], None, ALU.mult).then_inc(sums, 1)
                else:
                    nc.vector.scalar_tensor_tensor(out=dst, in0=src, scalar=acur[:, w, s:s + 1], in1=dst,
                                                   op0=ALU.mult, op1=ALU.add).then_inc(sums, 1)

            def last_waves(uu, U):
                w = uu // UNITS
                for a in range(2, NF):
                    s = SIN_ORDER[a]
                    v.wait_ge(sines, U * 5 + (a - 4 + SC))
                    v.wait_ge(sums, U * 5 + (a + AC - 6))
                    nc.vector.scalar_tensor_tensor(out=acc[:, uu % 2, :, :], in0=wave[:, a, :, :],
                                                   scalar=acur[:, w, s:s + 1], in1=acc[:, uu % 2, :, :],
                                                   op0=ALU.mult, op1=ALU.add).then_inc(sums, 1)

            def evacuate(w, n, i):
                v.wait_ge(products, n * UNITS + (VC - 1))
                v.wait_ge(stored[w], i * 64 + 16)
                nc.vector.tensor_copy(obuf[:, w, :], pv[:]).then_inc(evacs, 1)

            with v.Fori(0, NBH // BODY) as i:
                for uu in range(UNITS * BODY):
                    w, U = uu // UNITS, i * (UNITS * BODY) + uu
                    whole_turns(uu, V0, U, 0)
                    last_waves((uu - 1) % (UNITS * BODY), U)
                    whole_turns(uu, V2, U, 1)
                    if uu % UNITS == 1:
                        evacuate((w - 1) % 2, i * BODY + w, i)
                    if uu % UNITS == 0:
                        v.wait_ge(alpha_ready, i * BODY + (w + 1))
                    add_wave(uu, 0, U)
                    add_wave(uu, 1, U)
            last_waves(UNITS * BODY - 1, NBH * UNITS)
            evacuate(BODY - 1, NBH, NBH // BODY)


def stage_out0(nc, g):
    with ExitStack() as ctx:
        def sb(n, s, dt=F32):
            return ctx.enter_context(nc.sbuf_tensor(n, s, dt))
        num = sb("num", [P, 2, 2, QB])
        den = sb("den", [H0, 2, 2, QB])
        rden = sb("rden", [H0, 3, QB])
        tot = sb("tot", [P, 2, QB])
        aT = sb("aT", [P, 2, QB])
        wo, bo, sel = sb("wo", [P, D]), sb("bo", [1, D]), sb("sel", [H0, P])
        o = sb("o", [P, NT, D])
        st, mv, sd = sb("ost", [P, NT, 6]), sb("omv", [P, NT, 2]), sb("osd", [P, 3, NT])
        psb = ctx.enter_context(nc.psum_tensor("psb", [P, 2, QB], F32))
        pso = ctx.enter_context(nc.psum_tensor("pso", [P, 2, 4, D], F32))
        names = ("ow_in", "den1", "den2", "den3", "tot1", "bcast", "aT_done", "o_mm", "o_copied", "ostats",
                 "oaggr", "oveps", "oroot", "orinv", "onorm", "oscaled", "oadd")
        (w_in, den1, den2, den3, tot1, bcast, aT_done, o_mm, o_copied, stats, aggr, veps, root, rinv,
         onorm, oscaled, oadd) = sems(nc, g, *names)
        num_in = two(nc, g, "num_in")
        block = ctx.enter_context(nc.Block())

        @block.sync
        def _(sp):
            for dst, src in ((wo[:], g.src["wo0"]), (bo[:], g.src["bo0"]), (sel[:], g.src["k_sel"])):
                sp.dma_start(dst, src).then_inc(w_in, 16)
            for c in range(NC):
                b, qh = c // 2, c % 2
                rows = g.NUM[1 + H0 * b:1 + H0 * (b + 1)]
                if c >= 2:
                    sp.wait_ge(tot1, c - 1)
                    sp.wait_ge(den1, c - 1)
                for a in range(2):
                    sp.dma_start(num[:, c % 2, a, :],
                                 rows[:, 2 * qh + a, 0:HD0, :]).then_inc(num_in[c % 2], 16)
                    sp.dma_start(den[:, c % 2, a, :], rows[:, 2 * qh + a, HD0, :]).then_inc(num_in[c % 2], 16)

        @block.tensor
        def _(pe):
            pe.wait_ge(w_in, 48)
            for c in range(NC):
                pe.wait_ge(den3, c + 1)
                if c >= 2:
                    pe.wait_ge(aT_done, c - 1)
                nc.tensor.matmul(psb[:, c % 2, :], sel[:], rden[:, 2, :], start=True, stop=True).then_inc(bcast, 1)
                pe.wait_ge(aT_done, c + 1)
                if c >= 2:
                    pe.wait_ge(o_copied, c - 1)
                for k in range(4):
                    nc.tensor.matmul(pso[:, c % 2, k, :], aT[:, c % 2, P * k:P * (k + 1)], wo[:], start=True, stop=False)
                    last = nc.tensor.matmul(pso[:, c % 2, k, :], g.ones[0:1, :], bo[:], start=False, stop=True)
                last.then_inc(o_mm, 1)

        @block.scalar
        def _(act):
            for c in range(NC):
                act.wait_ge(o_mm, c + 1)
                nc.scalar.activation(o[:, 4 * c:4 * c + 4, :], pso[:, c % 2, :, :], ACT.Copy).then_inc(o_copied, 1)
            act.wait_ge(veps, 1)
            nc.scalar.activation(sd[:, 1, :], sd[:, 0, :], ACT.Sqrt).then_inc(root, 1)

        @block.vector
        def _(v):
            for c in range(NC):
                b = c // 2
                v.wait_ge(num_in[c % 2], 64 * (c // 2 + 1))
                if c >= 1:
                    v.wait_ge(bcast, c)
                nc.vector.scalar_tensor_tensor(out=rden[:, 0, :], in0=den[:, c % 2, 0, :], scalar=float(L),
                                               in1=den[:, c % 2, 1, :], op0=ALU.add, op1=ALU.add).then_inc(den1, 1)
                v.wait_ge(den1, c + 1)
                nc.vector.tensor_scalar(rden[:, 1, :], rden[:, 0, :], 2e-10, None, ALU.add).then_inc(den2, 1)
                v.wait_ge(den2, c + 1)
                nc.vector.reciprocal(rden[:, 2, :], rden[:, 1, :]).then_inc(den3, 1)
                nc.vector.scalar_tensor_tensor(out=tot[:, c % 2, :], in0=num[:, c % 2, 0, :], scalar=g.vsum[:, b:b + 1],
                                               in1=num[:, c % 2, 1, :], op0=ALU.add, op1=ALU.add).then_inc(tot1, 1)
                v.wait_ge(tot1, c + 1)
                v.wait_ge(bcast, c + 1)
                if c >= 2:
                    v.wait_ge(o_mm, c - 1)
                nc.vector.tensor_tensor(aT[:, c % 2, :], tot[:, c % 2, :], psb[:, c % 2, :], ALU.mult).then_inc(aT_done, 1)
            for t in range(NT):
                v.wait_ge(o_copied, t // 4 + 1)
                nc.vector.bn_stats(st[:, t, :], o[:, t, :]).then_inc(stats, 1)
            for t in range(NT):
                v.wait_ge(stats, t + 1)
                nc.vector.bn_aggr(mv[:, t, :], st[:, t, :]).then_inc(aggr, 1)
            v.wait_ge(aggr, NT)
            nc.vector.tensor_scalar(sd[:, 0, :], mv[:, :, 1], EPS, None, ALU.add).then_inc(veps, 1)
            v.wait_ge(root, 1)
            nc.vector.reciprocal(sd[:, 2, :], sd[:, 1, :]).then_inc(rinv, 1)
            v.wait_ge(rinv, 1)
            for b in range(B):
                for t in range(TB * b, TB * (b + 1)):
                    nc.vector.tensor_scalar(o[:, t, :], o[:, t, :], mv[:, t, 0:1], sd[:, 2, t:t + 1],
                                            ALU.subtract, ALU.mult).then_inc(onorm, 1)
                ob, xb = o[:, TB * b:TB * (b + 1), :], g.x[:, TB * b:TB * (b + 1), :]
                v.wait_ge(onorm, TB * (b + 1))
                nc.vector.tensor_tensor(ob, ob, g.bc[:, 0, b:b + 1, :].to_broadcast([P, TB, D]), ALU.mult).then_inc(oscaled, 1)
                v.wait_ge(oscaled, 2 * b + 1)
                nc.vector.tensor_tensor(ob, ob, g.bc[:, 1, b:b + 1, :].to_broadcast([P, TB, D]), ALU.add).then_inc(oscaled, 1)
                v.wait_ge(oscaled, 2 * b + 2)
                nc.vector.tensor_tensor(xb, xb, ob, ALU.add).then_inc(oadd, 1)
            v.wait_ge(oadd, B)


def stage_route0(nc, g):
    with ExitStack() as ctx:
        def sb(n, s, dt=F32):
            return ctx.enter_context(nc.sbuf_tensor(n, s, dt))
        wg, bg = sb("wg", [P, E0]), sb("bg", [1, E0])
        iot, tokid = sb("iot", [P, E0]), sb("tokid", [P, NT])
        tri, one = sb("tri", [P, P], BF16), sb("oneb", [P, P], BF16)
        lg, cand, ex, full = sb("lg", [P, NT, E0]), sb("cand", [P, NT, E0]), sb("ex", [P, NT, E0]), sb("full", [P, NT, E0])
        oneh = sb("oneh", [P, NT, E0], BF16)
        scan = sb("scan", [P, 2, NT, E0])
        col = sb("rcol", [P, 10, NT])
        zero = sb("zero", [P, 2048])
        psl = ctx.enter_context(nc.psum_tensor("psl", [P, NT, E0], F32))
        psp = ctx.enter_context(nc.psum_tensor("psp", [P, 2, NT, E0], F32))
        names = ("rw_in", "zeroed", "zero_out", "logits", "rstep", "exped", "counts", "low_done", "rows_out")
        w_in, zeroed, zero_out, logits, rstep, exped, counts, low_done, rows_out = sems(nc, g, *names)
        loads = [(wg[:], g.src["wg0"]), (bg[:], g.src["bg0"]), (iot[:], g.src["k_iota"]), (tokid[:], g.src["k_tok"]), (tri[:], g.src["k_tri"]), (one[:], g.src["k_one"])]
        block = ctx.enter_context(nc.Block())
        index_ready = [None]

        @block.sync
        def _(sp):
            for dst, src in loads:
                sp.dma_start(dst, src).then_inc(w_in, 16)
            sp.wait_ge(zeroed, 1)
            for k in range(2):
                sp.dma_start(g.ROWS[E0 * CAP // 2 * k:E0 * CAP // 2 * (k + 1), :].rearrange("(p r) d -> p (r d)", p=P),
                             zero[:]).then_inc(zero_out, 16)

        @block.tensor
        def _(pe):
            pe.wait_ge(w_in, 16 * len(loads))
            for t in range(NT):
                nc.tensor.matmul(psl[:, t, :], g.hT[:, P * t:P * (t + 1)], wg[:], start=True, stop=False)
                last = nc.tensor.matmul(psl[:, t, :], g.ones[0:1, :], bg[:], start=False, stop=True)
            last.then_inc(logits, 1)
            pe.wait_ge(rstep, 6)
            hot = oneh[:].rearrange("p t e -> p (t e)")
            nc.tensor.matmul(psp[:, 0].rearrange("p t e -> p (t e)"), tri[:], hot, start=True, stop=True)
            nc.tensor.matmul(psp[:, 1].rearrange("p t e -> p (t e)"), one[:], hot, start=True, stop=True).then_inc(counts, 1)

        @block.scalar
        def _(act):
            act.wait_ge(rstep, 3)
            nc.scalar.activation(ex[:], ex[:], ACT.Exp).then_inc(exped, 1)

        @block.vector
        def _(v):
            n = [0]
            nc.vector.memset(zero[:], 0.0).then_inc(zeroed, 1)
            v.wait_ge(w_in, 16 * len(loads))
            v.wait_ge(logits, 1)

            def done(ins):
                n[0] += 1
                ins.then_inc(rstep, 1)
                v.wait_ge(rstep, n[0])

            def wide(c):
                return c.rearrange("p (t o) -> p t o", o=1).to_broadcast([P, NT, E0])

            iob = iot[:].rearrange("p (o e) -> p o e", o=1).to_broadcast([P, NT, E0])
            top, low, eid, pos, keep, gate, posc, gi, si, den = [col[:, k, :] for k in range(10)]
            done(nc.vector.tensor_copy(lg[:], psl[:]))
            done(nc.vector.tensor_reduce(top, lg[:], AX.X, ALU.max))
            done(nc.vector.tensor_tensor(ex[:], lg[:], wide(top), ALU.subtract))
            done(nc.vector.tensor_tensor(cand[:], lg[:], wide(top), ALU.is_equal))
            done(nc.vector.scalar_tensor_tensor(out=full[:], in0=cand[:], scalar=-float(E0), in1=iob, op0=ALU.mult, op1=ALU.add))
            nc.vector.tensor_reduce(low, full[:], AX.X, ALU.min).then_inc(low_done, 1)
            v.wait_ge(low_done, 1)
            nc.vector.tensor_scalar(eid, low, float(E0), None, ALU.add).then_inc(low_done, 1)
            v.wait_ge(low_done, 2)
            done(nc.vector.tensor_tensor(oneh[:], iob, wide(eid), ALU.is_equal))
            v.wait_ge(exped, 1)
            done(nc.vector.tensor_reduce(den, ex[:], AX.X, ALU.add))
            done(nc.vector.reciprocal(gate, den))
            v.wait_ge(counts, 1)
            done(nc.vector.tensor_copy(scan[:, 0], psp[:, 1]))
            k = 0
            for s in (1, 2, 4, 8, 16):
                nc.vector.tensor_copy(scan[:, 1 - k, 0:s], scan[:, k, 0:s])
                done(nc.vector.tensor_tensor(scan[:, 1 - k, s:], scan[:, k, s:], scan[:, k, 0:NT - s], ALU.add))
                k = 1 - k
            nc.vector.tensor_copy(full[:, 0:1, :], psp[:, 0, 0:1, :])
            done(nc.vector.tensor_tensor(full[:, 1:, :], psp[:, 0, 1:, :], scan[:, k, 0:NT - 1, :], ALU.add))
            done(nc.vector.tensor_tensor(cand[:], full[:], oneh[:], ALU.mult))
            done(nc.vector.tensor_reduce(pos, cand[:], AX.X, ALU.add))
            done(nc.vector.tensor_scalar(keep, pos, float(CAP), None, ALU.is_lt))
            done(nc.vector.tensor_scalar(posc, pos, float(CAP - 1), None, ALU.min))
            done(nc.vector.scalar_tensor_tensor(out=gi, in0=eid, scalar=float(CAP), in1=posc, op0=ALU.mult, op1=ALU.add))
            done(nc.vector.tensor_copy(g.gidx[:], gi))
            done(nc.vector.tensor_tensor(si, gi, tokid[:], ALU.subtract))
            done(nc.vector.tensor_tensor(low, si, keep, ALU.mult))
            done(nc.vector.tensor_tensor(si, low, tokid[:], ALU.add))
            done(nc.vector.tensor_tensor(g.gate[:], gate, keep, ALU.mult))
            done(nc.vector.tensor_copy(g.sidx[:], si))
            index_ready[0] = n[0]

        @block.gpsimd
        def _(pool):
            pool.wait_ge(zero_out, 32)
            pool.wait_ge(rstep, index_ready[0])
            for t in range(NT):
                pool.indirect_dma_start(g.ROWS, bass.IndirectOffsetOnAxis(ap=g.sidx[:, t:t + 1], axis=0), g.h[:, t, :],
                                        None).then_inc(rows_out, 16)
            pool.wait_ge(rows_out, 16 * NT)


def stage_experts0(nc, g):
    NB = CAP // P
    NK = HF // P
    with ExitStack() as ctx:
        def sb(n, s, dt=F32):
            return ctx.enter_context(nc.sbuf_tensor(n, s, dt))
        rows, rowsT = sb("rows", [P, 2, NB, D]), sb("rowsT", [P, 2, CAP])
        w1, w2, b2 = sb("w1", [P, 2, HF]), sb("w2", [P, 2, NK, D]), sb("b2", [1, 2, D])
        b1 = sb("b1", [P, E0, NK])
        hid, y = sb("hid", [P, 2, NK, CAP]), sb("y", [P, 2, NB, D])
        ps_t = ctx.enter_context(nc.psum_tensor("ps_t", [P, 2, 512], F32))
        ps_h = ctx.enter_context(nc.psum_tensor("ps_h", [P, NK, CAP], F32))
        ps_y = ctx.enter_context(nc.psum_tensor("ps_y", [P, 2, 512], F32))
        b1_in, turned, rows_moved, hid_mm, hid_done, y_mm, y_moved, started = sems(
            nc, g, "b1_in", "turned", "rows_moved", "hid_mm", "hid_done", "y_mm", "y_moved", "started")
        expert_in, y_out = two(nc, g, "expert_in"), two(nc, g, "y_out")
        block = ctx.enter_context(nc.Block())
        W1, W2, B2 = g.src["w1"], g.src["w2"], g.src["b2"]
        ROWS = g.ROWS[0:E0 * CAP].rearrange("(e k p) d -> e p k d", e=E0, p=P)
        YR = g.Y.rearrange("(e k p) d -> e p k d", e=E0, p=P)

        @block.sync
        def _(sp):
            sp.dma_start(b1[:], g.src["b1"]).then_inc(b1_in, 16)
            with sp.Fori(0, E0 // 2) as i:
                for w in range(2):
                    e = i * 2 + w
                    sp.wait_ge(y_mm, e + 1)
                    sp.dma_start(rows[:, w, :, :], ROWS[e]).then_inc(expert_in[w], 16)
                    sp.dma_start(w1[:, w, :], W1[e]).then_inc(expert_in[w], 16)
                    sp.dma_start(w2[:, w, :, :], W2[e]).then_inc(expert_in[w], 16)
                    sp.dma_start(b2[:, w, :], B2[e]).then_inc(expert_in[w], 16)

        @block.tensor
        def _(pe):
            def first(e, w, i):
                pe.wait_ge(expert_in[w], i * 64 + 64)
                for k in range(NB):
                    last = nc.tensor.transpose(ps_t[:, w, P * k:P * (k + 1)], rows[:, w, k, :], g.ident[:])
                last.then_inc(turned, 1)
                pe.wait_ge(rows_moved, e + 1)
                pe.wait_ge(hid_done, e + 1)
                for c in range(NK):
                    last = nc.tensor.matmul(ps_h[:, c, :], w1[:, w, P * c:P * (c + 1)], rowsT[:, w, :], start=True, stop=True)
                last.then_inc(hid_mm, 1)

            def second(e, w):
                pe.wait_ge(hid_done, e + 2)
                for k in range(NB):
                    for c in range(NK):
                        nc.tensor.matmul(ps_y[:, w, D * k:D * (k + 1)], hid[:, w, c, P * k:P * (k + 1)], w2[:, w, c, :],
                                         start=(c == 0), stop=False)
                    last = nc.tensor.matmul(ps_y[:, w, D * k:D * (k + 1)], g.ones[0:1, :], b2[:, w, :], start=False, stop=True)
                last.then_inc(y_mm, 1)

            pe.wait_ge(started, 1)
            with pe.Fori(0, E0 // 2) as i:
                for w in range(2):
                    first(i * 2 + w, w, i)
                    second(i * 2 + w, w)

        @block.scalar
        def _(act):
            act.wait_ge(started, 1)
            with act.Fori(0, E0 // 2) as i:
                for w in range(2):
                    e = i * 2 + w
                    act.wait_ge(turned, e + 1)
                    nc.scalar.activation(rowsT[:, w, :], ps_t[:, w, 0:CAP], ACT.Copy).then_inc(rows_moved, 1)
                    act.wait_ge(y_mm, e + 3)
                    act.wait_ge(y_out[w], i * 16 + 16)
                    nc.scalar.activation(y[:, w, :, :], ps_y[:, w, 0:NB * D].rearrange("p (k d) -> p k d", k=NB),
                                         ACT.Copy).then_inc(y_moved, 1)
                    act.wait_ge(y_moved, e + 1)
                    act.dma_start(YR[e], y[:, w, :, :]).then_inc(y_out[w], 16)
            for w in range(2):
                act.wait_ge(y_out[w], 16 * (E0 // 2 + 1))

        @block.vector
        def _(v):
            v.memset(hid[:, 0, 0, 0:1], 0.0).then_inc(y_mm, 2)
            v.memset(hid[:, 0, 1, 0:1], 0.0).then_inc(hid_done, 1)
            for w in range(2):
                v.memset(hid[:, 1, w, 0:1], 0.0).then_inc(y_out[w], 16)
            v.memset(hid[:, 0, 2, 0:1], 0.0).then_inc(started, 1)
            v.wait_ge(started, 1)
            v.wait_ge(b1_in, 16)
            with v.Fori(0, E0 // 2) as i:
                for w in range(2):
                    e = i * 2 + w
                    v.wait_ge(hid_mm, e + 1)
                    for c in range(NK):
                        ins = nc.vector.tensor_scalar(hid[:, w, c, :], ps_h[:, c, :], b1[:, bass.ds(e, 1), c], 0.0,
                                                      ALU.add, ALU.max)
                    ins.then_inc(hid_done, 1)


def stage_combine0(nc, g):
    with ExitStack() as ctx:
        yg = ctx.enter_context(nc.sbuf_tensor("yg", [P, NT, D], F32))
        gathered, gated, scaled, added = sems(nc, g, "gathered", "gated", "scaled", "added")
        block = ctx.enter_context(nc.Block())

        @block.gpsimd
        def _(pool):
            for t in range(NT):
                pool.indirect_dma_start(yg[:, t, :], None, g.Y, bass.IndirectOffsetOnAxis(ap=g.gidx[:, t:t + 1], axis=0)
                                        ).then_inc(gathered, 16)

        @block.vector
        def _(v):
            v.wait_ge(gathered, 16 * NT)
            for b in range(B):
                for t in range(TB * b, TB * (b + 1)):
                    nc.vector.tensor_scalar(yg[:, t, :], yg[:, t, :], g.gate[:, t:t + 1], None, ALU.mult).then_inc(gated, 1)
                yb, xb = yg[:, TB * b:TB * (b + 1), :], g.x[:, TB * b:TB * (b + 1), :]
                v.wait_ge(gated, TB * (b + 1))
                nc.vector.tensor_tensor(yb, yb, g.bc[:, 4, b:b + 1, :].to_broadcast([P, TB, D]), ALU.mult).then_inc(scaled, 1)
                v.wait_ge(scaled, b + 1)
                nc.vector.tensor_tensor(xb, xb, yb, ALU.add).then_inc(added, 1)
            v.wait_ge(added, B)


def stage_attention1(nc, g):
    STEPS = B * TB * 2
    LAG_T, LAG_V = 2, 3
    NP = 4

    def step(t):
        return t // 16, t % 16 // 2, t % 2

    side = [(-1, "proj", 0, k) for k in range(8)]
    for t in range(STEPS + LAG_V):
        b, r = t // 16, t % 16
        if 4 <= r < 12 and b < B - 1:
            side.append((t, "proj", b + 1, r - 4))
        if b > 0 and r in (13, 14) and b < B:
            side.append((t, "wo", b - 1, r - 13))
    side += [(STEPS + LAG_V, "wo", B - 1, k) for k in range(2)]
    NS = len(side)

    with ExitStack() as ctx:
        def sb(n, s, dt=F32):
            return ctx.enter_context(nc.sbuf_tensor(n, s, dt))
        wqkv, wo = sb("wqkv", [P, 3, P]), sb("wo1", [P, D])
        qkv = sb("qkv", [P, 2, 3, L])
        vt = sb("vt", [P, 2, TB, P])
        pr = sb("pr", [P, NP, L])
        pT = sb("pT", [P, 2, TB, P])
        mx, nb, rs, ri = sb("mx", [P, NP]), sb("nb", [P, NP]), sb("rs", [P, NP]), sb("ri", [P, NP])
        cT = sb("cT", [P, 2, 2, QB])
        yT = sb("yT", [P, T])
        idb, mask = sb("idb", [P, P], BF16), sb("mask", [P, P], BF16)
        ps_s = ctx.enter_context(nc.psum_tensor("ps_s", [P, 2, L], F32))
        ps_t = ctx.enter_context(nc.psum_tensor("ps_t1", [P, TB, P], F32))
        ps_o = ctx.enter_context(nc.psum_tensor("ps_o", [P, QB], F32))
        ps_e = ctx.enter_context(nc.psum_tensor("ps_side", [P, QB], F32))
        (const_in, w_in, y_clear, side_mm, side_done, score_mm, maxed, shift, exped, inverse, normed, turned, moved,
         products, taken, scaled, turned_y, added) = sems(
            nc, g, "a_const_in", "a_w_in", "y_clear", "side_mm", "side_done", "score_mm", "maxed", "shift", "a_exped",
            "inverse", "normed", "a_turned", "a_moved", "a_products", "taken", "a_scaled", "turned_y", "a_added")
        block = ctx.enter_context(nc.Block())
        proj_uses = [n for n, s_ in enumerate(side) if s_[1] == "proj"]
        last_proj = proj_uses[-1] + 1

        def move(eng, seq, i, u):
            b, q, hh = step(u)
            seq.wait_ge(turned, i * STEPS + (u + 1))
            if u >= 2:
                seq.wait_ge(products, i * STEPS + (u - 1))
            dst, src = pT[:, u % 2, 0:q + 1, :], ps_t[:, 0:q + 1, :]
            if u % 2 == 0:
                nc.scalar.activation(dst, src, ACT.Copy).then_inc(moved, 1)
            else:
                nc.vector.tensor_copy(dst, src).then_inc(moved, 1)

        @block.sync
        def _(sp):
            sp.dma_start(idb[:], g.src["k_identb"]).then_inc(const_in, 16)
            sp.dma_start(mask[:], g.src["k_mask"]).then_inc(const_in, 16)
            with sp.Fori(0, HP) as i:
                sp.wait_ge(side_mm, i * NS + 1)
                sp.dma_start(wqkv[:], g.src["wqkv1"][i]).then_inc(w_in, 16)
                sp.dma_start(wo[:], g.src["wo1"][i]).then_inc(w_in, 16)

        @block.tensor
        def _(pe):
            pe.wait_ge(const_in, 32)

            def side_use(i, n):
                _, kind, b, k = side[n]
                pe.wait_ge(side_done, i * NS + (n + 1))
                if kind == "wo":
                    pe.wait_ge(taken, i * (2 * B) + (2 * b + k + 2))
                    last = nc.tensor.matmul(ps_e[:], wo[:], cT[:, b % 2, k, :], start=True, stop=True)
                elif k < 6:
                    last = nc.tensor.matmul(ps_e[:], wqkv[:, k // 2, :],
                                            g.hT[:, L * b + QB * (k % 2):L * b + QB * (k % 2 + 1)], start=True, stop=True)
                else:
                    for j in range(4):
                        c = QB * (k - 6) + P * j
                        last = nc.tensor.transpose(ps_e[:, P * j:P * (j + 1)], qkv[:, b % 2, 2, c:c + P], g.ident[:])
                last.then_inc(side_mm, 1)

            def scores(i, t):
                b, q, hh = step(t)
                if t % 16 == 0:
                    pe.wait_ge(side_done, i * NS + (proj_uses[8 * b + 7] + 2))
                if t >= 2:
                    pe.wait_ge(exped, i * STEPS + (t - 1))
                r, W = 64 * hh, P * (q + 1)
                lhs = qkv[r:r + HD1, b % 2, 0, P * q:P * (q + 1)]
                for c in range(0, W, QB):
                    hi = min(W, c + QB)
                    end = hi == W
                    last = nc.tensor.matmul(ps_s[:, t % 2, c:hi], lhs, qkv[r:r + HD1, b % 2, 1, c:hi], start=True,
                                            stop=not end, skip_group_check=True)
                last = nc.tensor.matmul(ps_s[:, t % 2, W - P:W], idb[:], mask[:], start=False, stop=True,
                                        skip_group_check=True)
                last.then_inc(score_mm, 1)

            def turn(i, t):
                b, q, hh = step(t)
                pe.wait_ge(normed, i * STEPS + (t + 1))
                if t >= 1:
                    pe.wait_ge(moved, i * STEPS + t)
                for j in range(q + 1):
                    last = nc.tensor.transpose(ps_t[:, j, :], pr[:, t % NP, P * j:P * (j + 1)], g.ident[:])
                last.then_inc(turned, 1)

            def value(i, t):
                b, q, hh = step(t)
                pe.wait_ge(moved, i * STEPS + (t + 1))
                if t % 8 == 0:
                    pe.wait_ge(taken, i * (2 * B) + (t // 8 + 1))
                r = 64 * hh
                for j in range(q + 1):
                    last = nc.tensor.matmul(ps_o[r:r + HD1, P * (q % 4):P * (q % 4 + 1)], vt[:, b % 2, j, r:r + HD1],
                                            pT[:, t % 2, j, :], start=(j == 0), stop=(j == q), skip_group_check=True)
                last.then_inc(products, 1)

            with pe.Fori(0, HP) as i:
                pe.wait_ge(w_in, i * 32 + 32)
                for n in range(8):
                    side_use(i, n)
                for t in range(STEPS + LAG_V):
                    if t < STEPS:
                        scores(i, t)
                    if LAG_T <= t < STEPS + LAG_T:
                        turn(i, t - LAG_T)
                    if t >= LAG_V:
                        value(i, t - LAG_V)
                    for n in range(8, NS):
                        if side[n][0] == t:
                            side_use(i, n)
                for n in range(NS - 2, NS):
                    side_use(i, n)
            for c in range(NC):
                pe.wait_ge(scaled, c + 1)
                if c >= 1:
                    pe.wait_ge(added, c)
                for k in range(4):
                    last = nc.tensor.transpose(ps_e[:, P * k:P * (k + 1)], yT[:, QB * c + P * k:QB * c + P * (k + 1)], g.ident[:])
                last.then_inc(turned_y, 1)

        @block.scalar
        def _(act):
            def side_take(i, n):
                _, kind, b, k = side[n]
                act.wait_ge(side_mm, i * NS + (n + 2))
                if k < 6:
                    dst = qkv[:, b % 2, k // 2, QB * (k % 2):QB * (k % 2 + 1)]
                else:
                    dst = vt[:, b % 2, 4 * (k - 6):4 * (k - 5), :].rearrange("p t d -> p (t d)")
                nc.scalar.activation(dst, ps_e[:], ACT.Copy).then_inc(side_done, 1)

            with act.Fori(0, HP) as i:
                for n in range(8):
                    side_take(i, n)
                for t in range(STEPS + LAG_V):
                    if t < STEPS:
                        b, q, hh = step(t)
                        W = P * (q + 1)
                        act.wait_ge(shift, i * STEPS + (t + 1))
                        if t >= NP:
                            act.wait_ge(turned, i * STEPS + (t - NP + 1))
                        nc.scalar.activation(pr[:, t % NP, 0:W], ps_s[:, t % 2, 0:W], ACT.Exp, bias=nb[:, t % NP:t % NP + 1],
                                             scale=float(HD1) ** -0.5, accum_out=rs[:, t % NP:t % NP + 1]).then_inc(exped, 1)
                    u = t - LAG_T
                    if 0 <= u < STEPS and u % 2 == 0:
                        move(nc.scalar, act, i, u)
                    for n in range(8, NS):
                        if side[n][0] == t and side[n][1] == "proj":
                            side_take(i, n)

        @block.gpsimd
        def _(pool):
            with pool.Fori(0, HP) as i:
                for t in range(STEPS):
                    b, q, hh = step(t)
                    pool.wait_ge(inverse, i * STEPS + (t + 1))
                    W = P * (q + 1)
                    nc.gpsimd.tensor_tensor(pr[:, t % NP, 0:W], pr[:, t % NP, 0:W],
                                            ri[:, t % NP:t % NP + 1].to_broadcast([P, W]), ALU.mult).then_inc(normed, 1)

        @block.vector
        def _(v):
            nc.vector.memset(yT[:], 0.0).then_inc(y_clear, 1)
            for k, count in enumerate((side_mm, side_done, taken)):
                nc.vector.memset(mx[:, k:k + 1], 0.0).then_inc(count, 1)
            v.wait_ge(y_clear, 1)

            def take(i, half):
                v.wait_ge(products, i * STEPS + 8 * (half + 1))
                b = half // 2
                if half >= 4:
                    n = [m for m, s_ in enumerate(side) if s_[1:] == ("wo", b - 2, half % 2)][0]
                    v.wait_ge(side_mm, i * NS + (n + 2))
                nc.vector.tensor_copy(cT[:, b % 2, half % 2, :], ps_o[:]).then_inc(taken, 1)

            def add_wo(i, n):
                _, _, b, k = side[n]
                v.wait_ge(side_mm, i * NS + (n + 2))
                dst = yT[:, L * b + QB * k:L * b + QB * (k + 1)]
                nc.vector.tensor_tensor(dst, ps_e[:], dst, ALU.add).then_inc(side_done, 1)

            with v.Fori(0, HP) as i:
                for t in range(STEPS + LAG_V + 1):
                    if t < STEPS:
                        b, q, hh = step(t)
                        v.wait_ge(score_mm, i * STEPS + (t + 1))
                        nc.vector.reduce_max(mx[:, t % NP:t % NP + 1], ps_s[:, t % 2, 0:P * (q + 1)], AX.X).then_inc(maxed, 1)
                        v.wait_ge(maxed, i * STEPS + (t + 1))
                        nc.vector.tensor_scalar(nb[:, t % NP:t % NP + 1], mx[:, t % NP:t % NP + 1], -float(HD1) ** -0.5, None,
                                                ALU.mult).then_inc(shift, 1)
                    if 1 <= t <= STEPS:
                        u = t - 1
                        v.wait_ge(exped, i * STEPS + (u + 1))
                        if u >= NP:
                            v.wait_ge(normed, i * STEPS + (u - NP + 1))
                        nc.vector.reciprocal(ri[:, u % NP:u % NP + 1], rs[:, u % NP:u % NP + 1]).then_inc(inverse, 1)
                    u = t - LAG_T
                    if 0 <= u < STEPS and u % 2 == 1:
                        move(nc.vector, v, i, u)
                    if t >= LAG_V + 8 and (t - LAG_V) % 8 == 0:
                        take(i, (t - LAG_V) // 8 - 1)
                    for n in range(8, NS):
                        if side[n][0] == t and side[n][1] == "wo" and t < STEPS + LAG_V:
                            add_wo(i, n)
                for n in range(NS - 2, NS):
                    add_wo(i, n)
            v.wait_ge(side_done, HP * NS + 1)
            for c in range(NC):
                b = c * QB // L
                nc.vector.tensor_scalar(yT[:, QB * c:QB * (c + 1)], yT[:, QB * c:QB * (c + 1)], g.mod[:, 1, 2, b:b + 1], None,
                                        ALU.mult).then_inc(scaled, 1)
                v.wait_ge(turned_y, c + 1)
                xc = g.x[:, 4 * c:4 * c + 4, :].rearrange("p t d -> p (t d)")
                nc.vector.tensor_tensor(xc, xc, ps_e[:], ALU.add).then_inc(added, 1)
            v.wait_ge(added, NC)


def stage_route1(nc, g):
    with ExitStack() as ctx:
        def sb(n, s, dt=F32):
            return ctx.enter_context(nc.sbuf_tensor(n, s, dt))
        wr, db, iot = sb("wr", [P, E1]), sb("db", [E1, D]), sb("iot1", [P, E1])
        lg = sb("lg1", [P, NT, E1])
        top, idx, idf = sb("top", [P, NT, 8]), sb("idx", [P, NT, 8], U32), sb("idf", [P, NT, 8])
        col = sb("col1", [P, 6, NT])
        hot, wt = sb("hot", [P, 2, NT, E1]), sb("wt1", [P, NT, E1])
        wT = sb("wT", [E1, T])
        psl = ctx.enter_context(nc.psum_tensor("psl1", [P, NT, E1], F32))
        psw = ctx.enter_context(nc.psum_tensor("psw", [E1, 2, QB], F32))
        psy = ctx.enter_context(nc.psum_tensor("psy1", [P, 2, 4, D], F32))
        w_in, logits, chain, exped, weights, turned, moved, bias_mm, bias_done, maxes = sems(
            nc, g, "r1_w_in", "r1_logits", "r1_chain", "r1_exped", "r1_weights", "r1_turned", "r1_moved", "r1_bias_mm",
            "r1_bias_done", "r1_maxes")
        loads = [(wr[:], g.src["wr1"]), (db[:], g.src["db1"]), (iot[:], g.src["k_iota"][:, 0:E1])]
        block = ctx.enter_context(nc.Block())

        @block.sync
        def _(sp):
            for dst, src in loads:
                sp.dma_start(dst, src).then_inc(w_in, 16)

        @block.tensor
        def _(pe):
            pe.wait_ge(w_in, 16 * len(loads))
            for t in range(NT):
                last = nc.tensor.matmul(psl[:, t, :], g.hT[:, P * t:P * (t + 1)], wr[:], start=True, stop=True)
            last.then_inc(logits, 1)
            pe.wait_ge(weights, 1)
            for c in range(NC):
                if c >= 2:
                    pe.wait_ge(moved, c - 1)
                for k in range(4):
                    last = nc.tensor.transpose(psw[:, c % 2, P * k:P * (k + 1)], wt[:, 4 * c + k, :], g.ident[:])
                last.then_inc(turned, 1)
                pe.wait_ge(moved, c + 1)
                if c >= 2:
                    pe.wait_ge(bias_done, c - 1)
                for k in range(4):
                    last = nc.tensor.matmul(psy[:, c % 2, k, :], wT[:, QB * c + P * k:QB * c + P * (k + 1)], db[:],
                                            start=True, stop=True)
                last.then_inc(bias_mm, 1)

        @block.scalar
        def _(act):
            act.wait_ge(chain, 3)
            nc.scalar.activation(col[:, 1, :], col[:, 0, :], ACT.Exp).then_inc(exped, 1)
            for c in range(NC):
                act.wait_ge(turned, c + 1)
                nc.scalar.activation(wT[:, QB * c:QB * (c + 1)], psw[:, c % 2, :], ACT.Copy).then_inc(moved, 1)

        @block.vector
        def _(v):
            n = [0]

            def done(ins):
                n[0] += 1
                ins.then_inc(chain, 1)
                v.wait_ge(chain, n[0])

            def wide(c):
                return c.rearrange("p (t o) -> p t o", o=1).to_broadcast([P, NT, E1])

            iob = iot[:].rearrange("p (o e) -> p o e", o=1).to_broadcast([P, NT, E1])
            v.wait_ge(w_in, 16 * len(loads))
            v.wait_ge(logits, 1)
            done(nc.vector.tensor_copy(lg[:], psl[:]))
            for t in range(NT):
                nc.vector.max(top[:, t, :], lg[:, t, :]).then_inc(maxes, 1)
            for t in range(NT):
                v.wait_ge(maxes, t + 1)
                nc.vector.max_index(idx[:, t, :], top[:, t, :], lg[:, t, :]).then_inc(maxes, 1)
            v.wait_ge(maxes, 2 * NT)
            done(nc.vector.tensor_copy(idf[:], idx[:]))
            done(nc.vector.tensor_tensor(col[:, 0, :], top[:, :, 1], top[:, :, 0], ALU.subtract))
            v.wait_ge(exped, 1)
            done(nc.vector.tensor_scalar(col[:, 2, :], col[:, 1, :], 1.0, None, ALU.add))
            done(nc.vector.reciprocal(col[:, 3, :], col[:, 2, :]))
            done(nc.vector.tensor_tensor(col[:, 4, :], col[:, 1, :], col[:, 3, :], ALU.mult))
            for k in range(2):
                done(nc.vector.tensor_tensor(hot[:, k], iob, wide(idf[:, :, k]), ALU.is_equal))
                done(nc.vector.tensor_tensor(hot[:, k], hot[:, k], wide(col[:, 3 + k, :]), ALU.mult))
            nc.vector.tensor_tensor(wt[:], hot[:, 0], hot[:, 1], ALU.add).then_inc(weights, 1)
            v.wait_ge(weights, 1)
            nc.vector.tensor_scalar(g.wexp[:], wt[:].rearrange("p t e -> p e t"), 1.0 / GALPHA, None, ALU.mult).then_inc(weights, 1)
            for c in range(NC):
                v.wait_ge(bias_mm, c + 1)
                nc.vector.tensor_copy(g.y[:, 4 * c:4 * c + 4, :], psy[:, c % 2, :, :]).then_inc(bias_done, 1)
            v.wait_ge(weights, 2)
            v.wait_ge(bias_done, NC)


def stage_experts1(nc, g):
    with ExitStack() as ctx:
        def sb(n, s, dt=F32):
            return ctx.enter_context(nc.sbuf_tensor(n, s, dt))
        gu, dn, gb = sb("gu", [P, 2, 2, I1]), sb("dn", [P, 2, D]), sb("gub", [P, 2, 2])
        bu1 = sb("bu1", [P, 2])
        gt, sil, up, hid = sb("gt", [P, 2, QB]), sb("sil", [P, 2, QB]), sb("up", [P, 2, QB]), sb("hid1", [P, 2, QB])
        ps_g = ctx.enter_context(nc.psum_tensor("ps_g", [P, 2, QB], F32))
        ps_u = ctx.enter_context(nc.psum_tensor("ps_u", [P, 2, QB], F32))
        ps_d = ctx.enter_context(nc.psum_tensor("ps_d", [P, 2, 4, D], F32))
        gate_mm, up_mm, gate_cut, silu, up_cut, hid_done, down_mm, summed, bias1, scaled, added = sems(
            nc, g, "x_gate_mm", "x_up_mm", "x_gate_cut", "x_silu", "x_up_cut", "x_hid", "x_down_mm", "x_summed",
            "x_bias1", "x_scaled", "x_added")
        expert_in = two(nc, g, "x_expert_in")
        block = ctx.enter_context(nc.Block())
        C0 = 2
        BC = 2 * NC

        @block.sync
        def _(sp):
            with sp.Fori(0, E1 // 2) as i:
                for w in range(2):
                    sp.wait_ge(down_mm, i * BC + (NC * w + 1))
                    e = i * 2 + w
                    sp.dma_start(gu[:, w, :, :], g.src["gu1"][e]).then_inc(expert_in[w], 16)
                    sp.dma_start(dn[:, w, :], g.src["dn1"][e]).then_inc(expert_in[w], 16)
                    sp.dma_start(gb[:, w, :], g.src["gub1"][e]).then_inc(expert_in[w], 16)

        @block.tensor
        def _(pe):
            def down(i, k):
                w, s = k // NC % 2, k % 2
                pe.wait_ge(hid_done, i * BC + (k + 1))
                pe.wait_ge(summed, i * BC + (k + 1))
                for j in range(4):
                    last = nc.tensor.matmul(ps_d[:, s, j, :], hid[:, s, P * j:P * (j + 1)], dn[:, w, :], start=True, stop=True)
                last.then_inc(down_mm, 1)

            with pe.Fori(0, E1 // 2) as i:
                for k in range(BC):
                    w, c, s = k // NC, k % NC, k % 2
                    if c == 0:
                        pe.wait_ge(expert_in[w], i * 48 + 48)
                    hc = g.hT[:, QB * c:QB * (c + 1)]
                    if k >= 2:
                        pe.wait_ge(gate_cut, i * BC + (k - 1))
                    nc.tensor.matmul(ps_g[:, s, :], gu[:, w, 0, :], hc, start=True, stop=True).then_inc(gate_mm, 1)
                    if k >= 2:
                        pe.wait_ge(up_cut, i * BC + (k - 1))
                    nc.tensor.matmul(ps_u[:, s, :], gu[:, w, 1, :], hc, start=True, stop=True).then_inc(up_mm, 1)
                    if k >= 1:
                        down(i, k - 1)
                down(i, BC - 1)

        @block.scalar
        def _(act):
            with act.Fori(0, E1 // 2) as i:
                for k in range(BC):
                    act.wait_ge(gate_cut, i * BC + (k + 1))
                    if k >= 2:
                        act.wait_ge(hid_done, i * BC + (k - 1))
                    nc.scalar.activation(sil[:, k % 2, :], gt[:, k % 2, :], ACT.Silu, scale=GALPHA).then_inc(silu, 1)

        @block.vector
        def _(v):
            v.memset(gt[:, 0, 0:1], 0.0).then_inc(down_mm, NC)
            v.memset(gt[:, 0, 1:2], 0.0).then_inc(summed, C0)

            def cuts(i, k):
                w, s = k // NC, k % 2
                if k % NC == 0:
                    v.wait_ge(expert_in[w], i * 48 + 48)
                    nc.vector.tensor_scalar(bu1[:, w:w + 1], gb[:, w, 1:2], 1.0, None, ALU.add).then_inc(bias1, 1)
                    v.wait_ge(bias1, i * 2 + (w + 1))
                v.wait_ge(gate_mm, i * BC + (k + 1))
                if k >= 2:
                    v.wait_ge(silu, i * BC + (k - 1))
                nc.vector.tensor_scalar(gt[:, s, :], ps_g[:, s, :], gb[:, w, 0:1], GLIM, ALU.add, ALU.min).then_inc(gate_cut, 1)
                v.wait_ge(up_mm, i * BC + (k + 1))
                nc.vector.tensor_scalar(up[:, s, :], ps_u[:, s, :], bu1[:, w:w + 1], 1.0 - GLIM, ALU.add, ALU.max).then_inc(up_cut, 1)

            def hidden(i, k):
                s = k % 2
                v.wait_ge(silu, i * BC + (k + 1))
                v.wait_ge(up_cut, i * BC + (k + 1))
                v.wait_ge(down_mm, i * BC + (k - 1 + NC))
                nc.vector.scalar_tensor_tensor(out=hid[:, s, :], in0=up[:, s, :], scalar=1.0 + GLIM, in1=sil[:, s, :],
                                               op0=ALU.min, op1=ALU.mult).then_inc(hid_done, 1)

            def total(i, k):
                w, c, s = k // NC, k % NC, k % 2
                v.wait_ge(down_mm, i * BC + (k + 1 + NC))
                v.wait_ge(summed, i * BC + (k + C0 - 1))
                for j in range(4):
                    t = 4 * c + j
                    last = nc.vector.scalar_tensor_tensor(out=g.y[:, t, :], in0=ps_d[:, s, j, :],
                                                          scalar=g.wexp[:, bass.ds(i * 2 + w, 1), t],
                                                          in1=g.y[:, t, :], op0=ALU.mult, op1=ALU.add)
                last.then_inc(summed, 1)

            with v.Fori(0, E1 // 2) as i:
                for k in range(BC):
                    cuts(i, k)
                    if k >= 1:
                        hidden(i, k - 1)
                    if k >= 2:
                        total(i, k - 2)
                hidden(i, BC - 1)
                total(i, BC - 2)
                total(i, BC - 1)
            v.wait_ge(summed, E1 * NC + C0)
            for b in range(B):
                yb, xb = g.y[:, TB * b:TB * (b + 1), :], g.x[:, TB * b:TB * (b + 1), :]
                nc.vector.tensor_tensor(yb, yb, g.bc[:, 5, b:b + 1, :].to_broadcast([P, TB, D]), ALU.mult).then_inc(scaled, 1)
                v.wait_ge(scaled, b + 1)
                nc.vector.tensor_tensor(xb, xb, yb, ALU.add).then_inc(added, 1)
            v.wait_ge(added, B)


def stage_store(nc, g):
    with ExitStack() as ctx:
        (out_done,) = sems(nc, g, "out_done")
        block = ctx.enter_context(nc.Block())

        @block.sync
        def _(sp):
            for b in range(B):
                sp.dma_start(g.out[L * b:L * (b + 1), :].rearrange("(t p) d -> p t d", p=P),
                             g.x[:, TB * b:TB * (b + 1), :]).then_inc(out_done, 16)
            sp.wait_ge(out_done, 16 * B)


def build(nc, a, out, stop=99):
    g = Ctx(a)
    g.out = out
    with ExitStack() as ctx:
        def sb(n, s, dt=F32):
            return ctx.enter_context(nc.sbuf_tensor(n, s, dt))

        def dram(n, s, dt=F32):
            return nc.dram_tensor(n, s, dt, kind="Internal").ap()
        g.x = sb("x", [P, NT, D])
        g.ident, g.ones = sb("ident", [P, P]), sb("ones", [P, P])
        g.gamma, g.beta = sb("gamma", [P, 1]), sb("beta", [P, 1])
        g.mod = sb("mod", [P, 2, 6, B])
        g.bc = sb("bc", [P, 6, B, D])
        g.KS = dram("ks", [NBH, 6, HD0, L], BF16)
        g.QS = dram("qs", [NBH, 3, HD0, NF, L], BF16)
        g.PH = dram("phd", [NBH, NF, 4, L], BF16)
        g.NUM = dram("numd", [NBH + 1, 4, HD0 + 1, QB])
        stage_mod(nc, g)
        with ExitStack() as c0:
          if START < 2:
            g.v9 = c0.enter_context(nc.sbuf_tensor("v9", [P, NBH, TB, HD0 + 1], F32))
            g.alpha = c0.enter_context(nc.sbuf_tensor("alpha", [P, NBH * NF], F32))
            g.vsum = c0.enter_context(nc.sbuf_tensor("vsum", [P, B], F32))
            with ExitStack() as c1:
                g.h = c1.enter_context(nc.sbuf_tensor("h0", [P, NT, D], F32))
                g.hT = c1.enter_context(nc.sbuf_tensor("hT0", [P, T], F32))
                stage_norm(nc, g, 0, 0, False)
                g.vtok = g.h
                stage_qkv0(nc, g)
            if stop > 1:
                stage_scores0(nc, g)
                stage_out0(nc, g)
        g.ROWS = dram("rowsd", [E0 * CAP + T, D])
        g.Y = dram("yd", [E0 * CAP, D])
        if stop > 2 and START < 3:
            with ExitStack() as c0:
                g.gate = c0.enter_context(nc.sbuf_tensor("gate", [P, NT], F32))
                g.gidx = c0.enter_context(nc.sbuf_tensor("gidx", [P, NT], U32))
                g.sidx = c0.enter_context(nc.sbuf_tensor("sidx", [P, NT], U32))
                with ExitStack() as c1:
                    g.h = c1.enter_context(nc.sbuf_tensor("h1", [P, NT, D], F32))
                    g.hT = c1.enter_context(nc.sbuf_tensor("hT1", [P, T], F32))
                    stage_norm(nc, g, 0, 3, True)
                    stage_route0(nc, g)
                stage_experts0(nc, g)
                stage_combine0(nc, g)
                clear_sems(nc, g)
        if stop > 3 and START < 4:
            with ExitStack() as c0:
                g.hT = c0.enter_context(nc.sbuf_tensor("hT2", [P, T], F32))
                with ExitStack() as c1:
                    g.h = c1.enter_context(nc.sbuf_tensor("h2", [P, NT, D], F32))
                    stage_norm(nc, g, 1, 0, False)
                stage_attention1(nc, g)
        if stop > 4:
            with ExitStack() as c0:
                g.hT = c0.enter_context(nc.sbuf_tensor("hT3", [P, T], F32))
                g.h = c0.enter_context(nc.sbuf_tensor("h3", [P, NT, D], F32))
                stage_norm(nc, g, 1, 3, False)
                g.y = g.h
                g.wexp = c0.enter_context(nc.sbuf_tensor("wexp", [P, E1, NT], F32))
                stage_route1(nc, g)
                stage_experts1(nc, g)
        stage_store(nc, g)


def host_arrays(i):
    f = np.ascontiguousarray
    r = np.arange(P)
    sel = (r[None, :] // HD0 == np.arange(H0)[:, None]).astype(np.float32)
    bf16 = np.dtype("bfloat16")
    mrow = np.zeros((P, QB), bf16)
    mrow[SROWS - 1] = MAGIC
    col = lambda a: f(a.reshape(-1, 1))
    wqkv = f(np.stack([i["L1_attn_" + n].reshape(HP, P, D).transpose(0, 2, 1) for n in ("wq", "wk", "wv")], axis=2))
    return {
        "x_d": f(i["L0_attn_x"].reshape(T, D)),
        "c0": f(i["L0_c"].T), "c1": f(i["L1_c"].T), "wm0": i["L0_wmod"], "wm1": i["L1_wmod"],
        "gamma_d": col(i["L0_attn_gamma"]), "beta_d": col(i["L0_attn_beta"]),
        "wq0": f(i["L0_attn_Wq"].T), "wk0": f(i["L0_attn_Wk"].T), "wv0": f(i["L0_attn_Wv"].T), "wo0": f(i["L0_attn_Wo"].T),
        "bq0": col(i["L0_attn_bq"]), "bk0": col(i["L0_attn_bk"]),
        "bv0": f(i["L0_attn_bv"].reshape(1, D)), "bo0": f(i["L0_attn_bo"].reshape(1, D)),
        "temp": f(i["L0_attn_temperature"].reshape(1, 1)), "phi": col(i["L0_attn_phi"]),
        "alpha_d": f(np.tile(i["L0_attn_alpha"].reshape(1, -1), (1, B))),
        "wg0": i["L0_ffn_Wg"], "bg0": f(i["L0_ffn_bg"].reshape(1, E0)), "w1": i["L0_ffn_W1"],
        "b1": f(i["L0_ffn_b1"].reshape(E0, HF // P, P).transpose(2, 0, 1)),
        "w2": f(i["L0_ffn_W2"].reshape(E0, HF // P, P, D).transpose(0, 2, 1, 3)), "b2": f(i["L0_ffn_b2"].reshape(E0, 1, D)),
        "wqkv1": wqkv, "wo1": f(i["L1_attn_wo"].T.reshape(HP, P, D)),
        "wr1": i["L1_ffn_router_weight"], "db1": i["L1_ffn_down_proj_bias"], "dn1": i["L1_ffn_down_proj"],
        "gu1": f(i["L1_ffn_gate_up_proj"].reshape(E1, D, I1, 2).transpose(0, 1, 3, 2)),
        "gub1": f(i["L1_ffn_gate_up_proj_bias"].reshape(E1, I1, 2)),
        "k_iota": np.tile(np.arange(E0, dtype=np.float32), (P, 1)),
        "k_tok": (E0 * CAP + np.arange(NT)[None, :] * P + r[:, None]).astype(np.float32),
        "k_tri": (r[:, None] < r[None, :]).astype(bf16), "k_one": np.ones((P, P), bf16),
        "k_identb": np.eye(P).astype(bf16),
        "k_mask": np.where(r[None, :] > r[:, None], NEG, 0.0).astype(bf16),
        "k_ident": np.eye(P, dtype=np.float32), "k_sel": sel, "k_mrow": mrow,
    }


def kernel(**inputs):
    import concourse.bacc as bacc
    from concourse.bass_utils import run_bass_kernel_spmd

    nc = bacc.Bacc("TRN2", target_bir_lowering=False, num_devices=1)
    arrays = host_arrays({k: np.asarray(v) for k, v in inputs.items()})
    aps = {k: nc.dram_tensor("in_" + k, a.shape, mybir.dt.from_np(a.dtype), kind="ExternalInput").ap() for k, a in arrays.items()}
    out = nc.dram_tensor("out_x", (T, D), F32, kind="ExternalOutput").ap()
    build(nc, aps, out)
    got = run_bass_kernel_spmd(nc, [{"in_" + k: a for k, a in arrays.items()}], core_ids=[0])
    return got.results[0]["out_x"].reshape(B, L, D)
```

```python
from contextlib import ExitStack

import numpy as np

import concourse.bass as bass
from concourse import mybir

ALU = mybir.AluOpType
ACT = mybir.ActivationFunctionType
AX = mybir.AxisListType
F32 = mybir.dt.float32
F16 = mybir.dt.float16
BF16 = mybir.dt.bfloat16
U32 = mybir.dt.uint32

P = 128
D = 128
B = 4
L = 1024
T = B * L
NT = T // P
TB = L // P
QB = 512
NC = T // QB
H0, HD0 = 16, 8
NF = 5
FREQS = [31.0, 37.0, 41.0, 43.0, 47.0]
NBH = B * H0
QROWS = 3 * HD0
KROWS = 6 * HD0
SROWS = KROWS + 4
MAGIC = 12582912.0
TURN = 6.283185005187988
EPS = 1e-5
E0, CAP, HF = 16, 256, 512
H1, HD1 = 16, 64
HP = H1 // 2
E1, I1 = 8, 128
GALPHA, GLIM = 1.702, 7.0
NEG = -1000000000.0


class Ctx:

    def __init__(self, arrays):
        self.src = arrays
        self.sems = []


def sems(nc, g, *names):
    got = [nc.alloc_semaphore(n) for n in names]
    g.sems += got
    return got


def clear_sems(nc, g):
    nc.clear_and_free_semaphores(g.sems)
    nc.all_engine_barrier()
    g.sems = []


def two(nc, g, name):
    return sems(nc, g, name + "_even", name + "_odd")


def stage_mod(nc, g):
    with ExitStack() as ctx:
        c_sb = ctx.enter_context(nc.sbuf_tensor("c_sb", [P, 2, B], F32))
        sc_sb = ctx.enter_context(nc.sbuf_tensor("sc_sb", [P, 2, B], F32))
        wm_sb = ctx.enter_context(nc.sbuf_tensor("wm_sb", [P, 2, 6 * D], F32))
        ps_mod = ctx.enter_context(nc.psum_tensor("ps_mod", [P, 2, 6, B], F32))
        ps_bc = ctx.enter_context(nc.psum_tensor("ps_bc", [P, 6, 4, D], F32))
        gab = ctx.enter_context(nc.sbuf_tensor("gab", [P, 4, 2, 2, B], F32))
        cols = ctx.enter_context(nc.sbuf_tensor("cols", [P, 6, B], F32))
        spread = ctx.enter_context(nc.sbuf_tensor("spread", [P, 6 * B, P], F32))
        small_in, x_in, silu_done, mod_mm, dve, cols_done, spread_done, bc_mm, bc_copied = sems(
            nc, g, "small_in", "x_in", "silu_done", "mod_mm", "mod_dve", "cols_done", "spread_done", "bc_mm", "bc_copied")
        small = [
            (c_sb[:, 0, :], g.src["c0"]), (c_sb[:, 1, :], g.src["c1"]), (wm_sb[:, 0, :], g.src["wm0"]), (wm_sb[:, 1, :], g.src["wm1"]),
            (g.ident[:], g.src["k_ident"]), (g.gamma[:], g.src["gamma_d"]), (g.beta[:], g.src["beta_d"]),
        ]
        block = ctx.enter_context(nc.Block())

        @block.sync
        def _(sp):
            for dst, src in small:
                sp.dma_start(dst, src).then_inc(small_in, 16)
            for k in range(4):
                sp.dma_start(g.x[:, TB * k:TB * (k + 1), :],
                             g.src["x_d"][L * k:L * (k + 1), :].rearrange("(t p) d -> p t d", p=P)).then_inc(x_in, 16)
            sp.wait_ge(x_in, 64)

        @block.scalar
        def _(act):
            act.wait_ge(small_in, 16 * len(small))
            nc.scalar.activation(sc_sb[:], c_sb[:], ACT.Silu).then_inc(silu_done, 1)

        @block.tensor
        def _(pe):
            pe.wait_ge(silu_done, 1)
            for y in range(2):
                for j in range(6):
                    last = nc.tensor.matmul(ps_mod[:, y, j, :], wm_sb[:, y, D * j:D * (j + 1)], sc_sb[:, y, :],
                                            start=True, stop=True)
            last.then_inc(mod_mm, 1)
            pe.wait_ge(spread_done, 6 * B)
            for n in range(6 * B):
                last = nc.tensor.matmul(ps_bc[:, n // 4, n % 4, :], spread[:, n, :], g.ident[:], start=True, stop=True)
            last.then_inc(bc_mm, 1)

        @block.vector
        def _(v):
            v.wait_ge(mod_mm, 1)
            nc.vector.tensor_copy(g.mod[:], ps_mod[:]).then_inc(dve, 1)
            v.wait_ge(dve, 1)
            for y in range(2):
                for j in (1, 4):
                    nc.vector.tensor_scalar(g.mod[:, y, j, :], g.mod[:, y, j, :], 1.0, None, ALU.add).then_inc(dve, 1)
                for k, j in enumerate((2, 5)):
                    nc.vector.tensor_scalar(gab[:, 0, y, k, :], g.mod[:, y, j, :], 0.0, 2.0, ALU.is_ge, ALU.mult).then_inc(dve, 1)
                    nc.vector.scalar_tensor_tensor(out=gab[:, 3, y, k, :], in0=g.mod[:, y, j, :], scalar=-1.0,
                                                   in1=g.mod[:, y, j, :], op0=ALU.mult, op1=ALU.max).then_inc(dve, 1)
            v.wait_ge(dve, 13)
            nc.vector.tensor_scalar(gab[:, 1], gab[:, 3], 0.25, None, ALU.max).then_inc(dve, 1)
            nc.vector.tensor_scalar(gab[:, 2], gab[:, 0], -1.0, None, ALU.add).then_inc(dve, 1)
            v.wait_ge(dve, 15)
            for k, j in enumerate((2, 5)):
                nc.vector.tensor_tensor(g.mod[:, :, j, :], gab[:, 1, :, k, :], gab[:, 2, :, k, :], ALU.mult).then_inc(dve, 1)
            v.wait_ge(dve, 17)
            nc.vector.tensor_scalar(cols[:, 0, :], g.mod[:, 0, 2, :], g.gamma[:, 0:1], None, ALU.mult).then_inc(cols_done, 1)
            nc.vector.tensor_scalar(cols[:, 1, :], g.mod[:, 0, 2, :], g.beta[:, 0:1], None, ALU.mult).then_inc(cols_done, 1)
            for k, (y, j) in enumerate(((0, 4), (0, 3), (0, 5), (1, 5))):
                nc.vector.tensor_copy(cols[:, 2 + k, :], g.mod[:, y, j, :]).then_inc(cols_done, 1)
            v.wait_ge(cols_done, 6)
            nc.vector.memset(g.ones[:], 1.0).then_inc(dve, 1)
            v.wait_ge(dve, 18)
            for n in range(6 * B):
                nc.vector.tensor_scalar(spread[:, n, :], g.ones[:], cols[:, n // B, n % B:n % B + 1], None,
                                        ALU.mult).then_inc(spread_done, 1)
            v.wait_ge(bc_mm, 1)
            nc.vector.tensor_copy(g.bc[:], ps_bc[:]).then_inc(bc_copied, 1)
            v.wait_ge(bc_copied, 1)


def stage_norm(nc, g, y, j, token_major):
    scale, shift = j + 1, j
    with ExitStack() as ctx:
        st = ctx.enter_context(nc.sbuf_tensor(f"st{y}{j}", [P, NT, 6], F32))
        mv = ctx.enter_context(nc.sbuf_tensor(f"mv{y}{j}", [P, NT, 2], F32))
        sd = ctx.enter_context(nc.sbuf_tensor(f"sd{y}{j}", [P, 3, NT], F32))
        psT = ctx.enter_context(nc.psum_tensor(f"psT{y}{j}", [P, NC, QB], F32))
        h = g.h
        stats, aggr, veps, root, rinv, hn, hmod, turned, moved = sems(
            nc, g, *[f"n{y}{j}_{s}" for s in ("stats", "aggr", "veps", "root", "rinv", "hn", "hmod", "turned", "moved")])
        block = ctx.enter_context(nc.Block())

        @block.vector
        def _(v):
            for t in range(NT):
                nc.vector.bn_stats(st[:, t, :], g.x[:, t, :]).then_inc(stats, 1)
            for t in range(NT):
                v.wait_ge(stats, t + 1)
                nc.vector.bn_aggr(mv[:, t, :], st[:, t, :]).then_inc(aggr, 1)
            v.wait_ge(aggr, NT)
            nc.vector.tensor_scalar(sd[:, 0, :], mv[:, :, 1], EPS, None, ALU.add).then_inc(veps, 1)
            v.wait_ge(root, 1)
            nc.vector.reciprocal(sd[:, 2, :], sd[:, 1, :]).then_inc(rinv, 1)
            v.wait_ge(rinv, 1)
            for t in range(NT):
                nc.vector.tensor_scalar(h[:, t, :], g.x[:, t, :], mv[:, t, 0:1], sd[:, 2, t:t + 1],
                                        ALU.subtract, ALU.mult).then_inc(hn, 1)
                if token_major and t % TB == TB - 1:
                    b = t // TB
                    hb = h[:, TB * b:TB * (b + 1), :]
                    v.wait_ge(hn, t + 1)
                    nc.vector.tensor_tensor(hb, hb, g.bc[:, 2, b:b + 1, :].to_broadcast([P, TB, D]),
                                            ALU.mult).then_inc(hmod, 1)
                    v.wait_ge(hmod, 2 * b + 1)
                    nc.vector.tensor_tensor(hb, hb, g.bc[:, 3, b:b + 1, :].to_broadcast([P, TB, D]),
                                            ALU.add).then_inc(hmod, 1)

        @block.scalar
        def _(act):
            act.wait_ge(veps, 1)
            nc.scalar.activation(sd[:, 1, :], sd[:, 0, :], ACT.Sqrt).then_inc(root, 1)
            for c in range(NC):
                b = c * QB // L
                act.wait_ge(turned, c + 1)
                if token_major:
                    nc.scalar.activation(g.hT[:, c * QB:(c + 1) * QB], psT[:, c, :], ACT.Copy).then_inc(moved, 1)
                else:
                    nc.scalar.activation(g.hT[:, c * QB:(c + 1) * QB], psT[:, c, :], ACT.Identity,
                                         bias=g.mod[:, y, shift, b:b + 1],
                                         scale=g.mod[:, y, scale, b:b + 1]).then_inc(moved, 1)
            act.wait_ge(moved, NC)

        @block.tensor
        def _(pe):
            for c in range(NC):
                if token_major:
                    pe.wait_ge(hmod, 2 * (c * QB // L) + 2)
                else:
                    pe.wait_ge(hn, 4 * c + 4)
                for k in range(4):
                    last = nc.tensor.transpose(psT[:, c, P * k:P * (k + 1)], h[:, 4 * c + k, :], g.ident[:])
                last.then_inc(turned, 1)


def stage_qkv0(nc, g):
    NQ = 4
    with ExitStack() as ctx:
        def sb(n, s, dt=F32):
            return ctx.enter_context(nc.sbuf_tensor(n, s, dt))
        wq, wk, wv, cb, bvr = sb("wq", [P, D]), sb("wk", [P, D]), sb("wv", [P, D]), sb("cb", [P, 8]), sb("bvr", [1, D])
        ph = sb("ph", [NF * H0, 8])
        pb = sb("pb", [NF * H0, 4], BF16)
        phr = sb("phr", [NF * H0, 4, L], BF16)
        one80 = sb("one80", [NF * H0, L])
        q_sb, k_sb = sb("q_sb", [P, 2, QB]), sb("k_sb", [P, 2, QB])
        res = sb("res", [P, 2, QB])
        qp = sb("qp", [P, NQ, 3, QB], BF16)
        kp = sb("kp", [P, 2, 3, QB], BF16)
        psq = ctx.enter_context(nc.psum_tensor("psq", [P, 2, QB], F32))
        psk = ctx.enter_context(nc.psum_tensor("psk", [P, 2, QB], F32))
        psv = ctx.enter_context(nc.psum_tensor("psv", [P, 2, 4, D], F32))
        pss = ctx.enter_context(nc.psum_tensor("pss", [P, B], F32))
        (w_in, scale_d, phase_d, ph_out, q_mm, k_mm, v_mm, q_copied, k_copied, v_copied, hi_d, res_d, mid_d, lo_d,
         khi_d, kmid_d, klo_d, s_mm, s_copied, vset) = sems(
            nc, g, "w_in", "scale_d", "phase_d", "ph_out", "q_mm", "k_mm", "v_mm", "q_copied", "k_copied", "v_copied",
            "hi_d", "res_d", "mid_d", "lo_d", "khi_d", "kmid_d", "klo_d", "s_mm", "s_copied", "vset")
        q_out, k_out = sems(nc, g, *["q_out%d" % k for k in range(NQ)]), two(nc, g, "k_out")
        loads = [(wq[:], g.src["wq0"]), (wk[:], g.src["wk0"]), (wv[:], g.src["wv0"]), (cb[:, 0:1], g.src["bq0"]), (cb[:, 1:2], g.src["bk0"]), (bvr[:], g.src["bv0"]),
                 (cb[:, 2:3], g.src["temp"].to_broadcast([P, 1])), (ph[:, 0:1], g.src["phi"]),
                 (g.alpha[:], g.src["alpha_d"].to_broadcast([P, NBH * NF]))]
        block = ctx.enter_context(nc.Block())

        @block.sync
        def _(sp):
            for dst, src in loads:
                sp.dma_start(dst, src).then_inc(w_in, 16)
            sp.wait_ge(phase_d, 10)
            for b in range(B):
                sp.dma_start(g.PH[H0 * b:H0 * (b + 1)].rearrange("h f r n -> (h f) r n"), phr[:]).then_inc(ph_out, 16)
            for c in range(NC):
                b, col = c * QB // L, c * QB % L
                sp.wait_ge(klo_d, c + 1)
                for row, part in enumerate((0, 0, 0, 1, 1, 2)):
                    sp.dma_start(g.KS[H0 * b:H0 * (b + 1), row, :, col:col + QB],
                                 kp[:, c % 2, part, :]).then_inc(k_out[c % 2], 16)
                for f in range(NF):
                    m = c * NF + f
                    sp.wait_ge(lo_d, m + 1)
                    for part in range(3):
                        sp.dma_start(g.QS[H0 * b:H0 * (b + 1), part, :, f, col:col + QB],
                                     qp[:, m % NQ, part, :]).then_inc(q_out[m % NQ], 16)
            sp.wait_ge(ph_out, 16 * B)
            for k in range(2):
                sp.wait_ge(k_out[k], 16 * 6 * NC // 2)
            for k in range(NQ):
                sp.wait_ge(q_out[k], 16 * 3 * NF * NC // NQ)

        @block.tensor
        def _(pe):
            pe.wait_ge(w_in, 16 * len(loads))
            for c in range(NC):
                hc = g.hT[:, c * QB:(c + 1) * QB]
                if c >= 2:
                    pe.wait_ge(q_copied, c - 1)
                nc.tensor.matmul(psq[:, c % 2, :], wq[:], hc, start=True, stop=True).then_inc(q_mm, 1)
                if c >= 2:
                    pe.wait_ge(k_copied, c - 1)
                nc.tensor.matmul(psk[:, c % 2, :], wk[:], hc, start=True, stop=True).then_inc(k_mm, 1)
                if c >= 2:
                    pe.wait_ge(v_copied, c - 1)
                for k in range(4):
                    nc.tensor.matmul(psv[:, c % 2, k, :], hc[:, P * k:P * (k + 1)], wv[:], start=True, stop=False)
                    last = nc.tensor.matmul(psv[:, c % 2, k, :], g.ones[0:1, :], bvr[:], start=False, stop=True)
                last.then_inc(v_mm, 1)
            pe.wait_ge(v_copied, NC)
            pe.wait_ge(vset, 1)
            for b in range(B):
                for t in range(TB):
                    last = nc.tensor.matmul(pss[:, b:b + 1], g.vtok[:, TB * b + t, :], g.ones[:, 0:1],
                                            start=(t == 0), stop=(t == TB - 1))
            last.then_inc(s_mm, 1)

        @block.scalar
        def _(act):
            act.wait_ge(scale_d, 4)
            for c in range(NC):
                act.wait_ge(v_mm, c + 1)
                nc.scalar.activation(g.vtok[:, 4 * c:4 * c + 4, :], psv[:, c % 2, :, :], ACT.Copy).then_inc(v_copied, 1)
                act.wait_ge(k_copied, c + 1)
                if c >= 2:
                    act.wait_ge(k_out[c % 2], 16 * 6 * (c // 2))
                nc.scalar.activation(kp[:, c % 2, 0, :], k_sb[:, c % 2, :], ACT.Copy).then_inc(khi_d, 1)
                for f in range(NF):
                    m = c * NF + f
                    act.wait_ge(q_copied, c + 1)
                    if m >= NQ:
                        act.wait_ge(q_out[m % NQ], 16 * 3 * (m // NQ))
                    nc.scalar.activation(qp[:, m % NQ, 0, :], q_sb[:, c % 2, :], ACT.Copy, scale=1.0 / FREQS[f]).then_inc(hi_d, 1)

        @block.vector
        def _(v):
            v.wait_ge(w_in, 16 * len(loads))
            nc.vector.scalar_tensor_tensor(out=cb[:, 3:4], in0=cb[:, 2:3], scalar=-1.0, in1=cb[:, 2:3], op0=ALU.mult,
                                           op1=ALU.max).then_inc(scale_d, 1)
            v.wait_ge(scale_d, 1)
            nc.vector.tensor_scalar(cb[:, 4:5], cb[:, 3:4], 0.1, float(np.sqrt(HD0)), ALU.add, ALU.mult).then_inc(scale_d, 1)
            v.wait_ge(scale_d, 2)
            nc.vector.reciprocal(cb[:, 5:6], cb[:, 4:5]).then_inc(scale_d, 1)
            v.wait_ge(scale_d, 3)
            steps = [
                lambda: nc.vector.tensor_scalar(ph[:, 1:2], ph[:, 0:1], float(1 / (2 * np.pi)), None, ALU.mult),
                lambda: nc.vector.tensor_scalar(ph[:, 2:3], ph[:, 1:2], MAGIC, -MAGIC, ALU.add, ALU.add),
                lambda: nc.vector.tensor_tensor(ph[:, 3:4], ph[:, 1:2], ph[:, 2:3], ALU.subtract),
                lambda: nc.vector.tensor_copy(pb[:, 0:1], ph[:, 3:4]),
                lambda: nc.vector.tensor_tensor(ph[:, 4:5], ph[:, 3:4], pb[:, 0:1], ALU.subtract),
                lambda: nc.vector.tensor_copy(pb[:, 1:2], ph[:, 4:5]),
                lambda: nc.vector.tensor_tensor(ph[:, 5:6], ph[:, 4:5], pb[:, 1:2], ALU.subtract),
            ]
            nc.vector.memset(one80[:], 1.0).then_inc(scale_d, 1)
            for n, step in enumerate(steps):
                step().then_inc(phase_d, 1)
                v.wait_ge(phase_d, n + 1)
            v.wait_ge(scale_d, 4)
            for r, src in enumerate((ph[:, 3:4], ph[:, 4:5], ph[:, 5:6])):
                ins = nc.vector.tensor_scalar(phr[:, r, :], one80[:], src, None, ALU.mult)
                if r < 2:
                    ins.then_inc(phase_d, 1)
            nc.vector.memset(phr[:, 3, :], 0.0).then_inc(phase_d, 1)
            for c in range(NC):
                v.wait_ge(q_mm, c + 1)
                if c >= 2:
                    v.wait_ge(hi_d, NF * (c - 1))
                nc.vector.tensor_scalar(q_sb[:, c % 2, :], psq[:, c % 2, :], cb[:, 0:1], cb[:, 5:6],
                                        ALU.add, ALU.mult).then_inc(q_copied, 1)
                v.wait_ge(k_mm, c + 1)
                if c >= 2:
                    v.wait_ge(khi_d, c - 1)
                nc.vector.tensor_scalar(k_sb[:, c % 2, :], psk[:, c % 2, :], cb[:, 1:2], None, ALU.add).then_inc(k_copied, 1)
                v.wait_ge(khi_d, c + 1)
                nc.vector.tensor_tensor(res[:, (c + c * NF) % 2, :], k_sb[:, c % 2, :], kp[:, c % 2, 0, :],
                                        ALU.subtract).then_inc(res_d, 1)
                v.wait_ge(res_d, c + c * NF + 1)
                nc.vector.tensor_copy(kp[:, c % 2, 1, :], res[:, (c + c * NF) % 2, :]).then_inc(kmid_d, 1)
                v.wait_ge(kmid_d, c + 1)
                nc.vector.tensor_tensor(kp[:, c % 2, 2, :], res[:, (c + c * NF) % 2, :], kp[:, c % 2, 1, :],
                                        ALU.subtract).then_inc(klo_d, 1)
                for f in range(NF):
                    m = c * NF + f
                    r = (c + m + 1) % 2
                    v.wait_ge(hi_d, m + 1)
                    nc.vector.scalar_tensor_tensor(out=res[:, r, :], in0=q_sb[:, c % 2, :], scalar=1.0 / FREQS[f],
                                                   in1=qp[:, m % NQ, 0, :], op0=ALU.mult, op1=ALU.subtract).then_inc(res_d, 1)
                    v.wait_ge(res_d, c + m + 2)
                    nc.vector.tensor_copy(qp[:, m % NQ, 1, :], res[:, r, :]).then_inc(mid_d, 1)
                    v.wait_ge(mid_d, m + 1)
                    nc.vector.tensor_tensor(qp[:, m % NQ, 2, :], res[:, r, :], qp[:, m % NQ, 1, :], ALU.subtract).then_inc(lo_d, 1)
            v.wait_ge(s_mm, 1)
            nc.vector.tensor_copy(g.vsum[:], pss[:]).then_inc(s_copied, 1)
            v.wait_ge(s_copied, 1)

        @block.gpsimd
        def _(pool):
            nc.gpsimd.memset(g.v9[:], 1.0).then_inc(vset, 1)
            pool.wait_ge(vset, 1)
            pool.wait_ge(v_copied, NC)
            for b in range(B):
                last = nc.gpsimd.tensor_copy(g.v9[:, H0 * b:H0 * (b + 1), :, 0:HD0].rearrange("p h t d -> p t h d"),
                                             g.vtok[:, TB * b:TB * (b + 1), :].rearrange("p t (h d) -> p t h d", h=H0))
            last.then_inc(vset, 1)
            pool.wait_ge(vset, 2)


V0, P1, P3, V2, P4 = range(5)
SIN_ORDER = [P1, V0, P3, P4, V2]
SLOTS = 3
UNITS = 8
BODY = 2


def slot_plan():
    swapped = (5, 10)
    steps = [(u, s) for u in range(UNITS * BODY) for s in range(NF)]
    total = NF * UNITS * BODY
    read = [k - SLOTS for k in range(SLOTS)]
    slot, after = {}, {}
    for u, s in steps:
        by_reading = sorted(range(SLOTS), key=lambda j: read[j])
        slot[(u, s)] = k = by_reading[1 if s == V2 and u in swapped else 0]
        read[k] = NF * u + SIN_ORDER.index(s)
    read = [q - total for q in read]
    assert read == sorted(read)
    for u, s in steps:
        k = slot[(u, s)]
        after[(u, s)], read[k] = read[k], NF * u + SIN_ORDER.index(s)
    return slot, after


def stage_scores0(nc, g):
    SC, FC, AC, TC, VC, OC = 6, 2, 36, 3, 12, 2
    SUMS = NF - 1
    slot, after = slot_plan()
    with ExitStack() as ctx:
        def sb(n, s, dt=F32):
            return ctx.enter_context(nc.sbuf_tensor(n, s, dt))
        qst = sb("qst", [P, 2, NF, L], BF16)
        kst = sb("kst", [P, 2, L], BF16)
        kneg = sb("kneg", [P, 2, L], BF16)
        nil = sb("nil", [P, L], BF16)
        mrow = sb("mrow", [P, QB], BF16)
        negi = sb("negi", [P, P], F16)
        vcur = sb("vcur", [P, 2, TB, 32])
        acur = sb("acur", [P, 2, NF])
        turns = sb("turns", [P, 2, 2, QB], F16)
        wave = sb("wave", [P, NF, 2, QB])
        acc = sb("acc", [P, 2, 2, QB])
        wt = sb("wt", [P, 2, 2, QB])
        obuf = sb("obuf", [P, 2, QB])
        credit = sb("credit", [P, 10])
        ps = ctx.enter_context(nc.psum_tensor("ps_steps", [P, SLOTS, 2, QB], F32))
        pv = ctx.enter_context(nc.psum_tensor("ps_pv", [P, QB], F32))
        (cleared, stack_used, kneg_ready, v_ready, alpha_ready, raw_ready, turns_ready, angle_ready,
         sines, firsts, sums, tanhs, products, evacs, pv_cleared, mrow_in, silu_loaded) = sems(
            nc, g, "cleared", "stack_used", "kneg_ready", "v_ready", "alpha_ready", "raw_ready",
            "turns_ready", "angle_ready", "sines", "firsts", "sums", "tanhs", "products", "evacs", "pv_cleared", "mrow_in", "silu_loaded")
        stack_in, stored = two(nc, g, "stack_in"), two(nc, g, "stored")
        CLEAR = 12
        block = ctx.enter_context(nc.Block())
        NLOAD = 5

        @block.sync
        def _(sp):
            sp.dma_start(mrow[:], g.src["k_mrow"]).then_inc(mrow_in, 16)
            sp.wait_ge(cleared, CLEAR)
            with sp.Fori(0, NBH // BODY) as i:
                for w in range(BODY):
                    n = i * BODY + w
                    sp.wait_ge(stack_used, n + 1)
                    for lo, k in ((0, 3), (3 * HD0, 2), (5 * HD0, 1)):
                        sp.dma_start(qst[lo:lo + k * HD0, w, :, :],
                                     g.QS[n, 0:k].rearrange("k d f n -> (k d) f n")).then_inc(stack_in[w], 16)
                    sp.dma_start(qst[KROWS:SROWS, w, :, :], g.PH[n].rearrange("f r n -> r f n")).then_inc(stack_in[w], 16)
                    sp.dma_start(kst[0:KROWS, w, :], g.KS[n].rearrange("k d n -> (k d) n")).then_inc(stack_in[w], 16)

        @block.gpsimd
        def _(pool):
            pool.memset(kst[:], 1.0).then_inc(cleared, 1)
            pool.memset(kneg[:], 1.0).then_inc(cleared, 1)
            pool.memset(qst[:], 0.0).then_inc(cleared, 1)
            pool.memset(vcur[:], 0.0).then_inc(cleared, 1)
            pool.memset(acur[:], 0.0).then_inc(cleared, 1)
            pool.memset(nil[:], 0.0).then_inc(cleared, 1)
            pool.wait_ge(cleared, CLEAR)

            def prepare(w, n, stacks):
                pool.wait_ge(products, n * UNITS + (VC - UNITS - 1))
                nc.gpsimd.tensor_copy(vcur[:, w, :, 0:HD0 + 1], g.v9[:, bass.ds(n, 1), :, :].rearrange(
                    "p o t d -> p (o t) d")).then_inc(v_ready, 1)
                pool.wait_ge(sums, n * (SUMS * UNITS) + (AC - SUMS * UNITS - 1))
                nc.gpsimd.tensor_copy(acur[:, w, :], g.alpha[:, bass.ds(n * NF, NF)]).then_inc(alpha_ready, 1)
                pool.wait_ge(stack_in[w], stacks * (16 * NLOAD))
                nc.gpsimd.tensor_tensor(kneg[:, w, :], nil[:], kst[:, w, :], ALU.subtract).then_inc(kneg_ready, 1)

            def first_terms(i, last):
                for uu in range(UNITS * BODY):
                    w, U = uu // UNITS, i * (UNITS * BODY) + uu
                    if uu % UNITS == 0:
                        pool.wait_ge(alpha_ready, i * BODY + (w + 1))
                    pool.wait_ge(sines, U * NF + SC)
                    pool.wait_ge(tanhs, U + (TC - 2))
                    s = SIN_ORDER[0]
                    nc.gpsimd.tensor_tensor(acc[:, uu % 2, :, :].rearrange("p a q -> p (a q)"),
                                            wave[:, 0, :, :].rearrange("p a q -> p (a q)"),
                                            acur[:, w, s:s + 1].to_broadcast([P, 2 * QB]), ALU.mult).then_inc(firsts, 1)
                    if uu % UNITS == UNITS // 2 and not (last and w == BODY - 1):
                        prepare((w + 1) % BODY, i * BODY + (w + 1), i + (w + 1) // BODY + 1)

            prepare(0, 0, 1)
            with pool.Fori(0, NBH // BODY - 1) as i:
                first_terms(i, False)
            first_terms(NBH // BODY - 1, True)

        def pv_product(pe, prev_w, uu, U, n_prev, head_done=False):
            jp, qh = uu % UNITS // 2, uu % 2
            pe.wait_ge(tanhs, U + (TC - 1))
            if jp == 0:
                pe.wait_ge(evacs, n_prev + (OC - 1))
                if qh == 0:
                    pe.wait_ge(v_ready, n_prev + 1)
            for a in range(2):
                r = 32 * (2 * qh + a)
                last = nc.tensor.matmul(pv[r:r + 32, :], vcur[:, prev_w, 2 * jp + a, :], wt[:, uu % 2, a, :],
                                        start=(jp == 0), stop=(jp == 3), skip_group_check=True)
                if a == 0 and head_done:
                    last.then_inc(stack_used, 1)
            last.then_inc(products, 1)

        @block.tensor
        def _(pe):
            pe.wait_ge(cleared, CLEAR)
            pe.wait_ge(mrow_in, 16)
            for r in range(0, P, 32):
                last = nc.tensor.matmul(pv[r:r + 32, :], vcur[:, BODY - 1, 0, :], wt[:, 1, 0, :], start=True, stop=True,
                                        skip_group_check=True)
            last.then_inc(pv_cleared, 1)

            def angles(w, uu, s, neg, mag, start):
                jp, qh = uu % UNITS // 2, uu % 2
                for a in range(2):
                    j = 2 * jp + a
                    k = (kneg if neg else kst)[:, w, P * j:P * (j + 1)]
                    q = mrow[:] if mag else qst[:, w, s, QB * qh:QB * (qh + 1)]
                    last = nc.tensor.matmul(ps[:, slot[(uu, s)], a, :], k, q, start=start,
                                            stop=not neg and not mag, skip_group_check=True)
                return last

            def less_turns(uu, s, k):
                for a in range(2):
                    last = nc.tensor.matmul(ps[:, slot[(uu, s)], a, :], negi[:], turns[:, k, a, :], start=False,
                                            stop=True, skip_group_check=True)
                return last

            with pe.Fori(0, NBH // BODY) as i:
                for uu in range(UNITS * BODY):
                    w, n, U = uu // UNITS, i * BODY + uu // UNITS, i * (UNITS * BODY) + uu
                    if uu % UNITS == 0:
                        pe.wait_ge(stack_in[w], i * (16 * NLOAD) + 16 * NLOAD)
                        pe.wait_ge(kneg_ready, n + 1)

                    def slot_free(s):
                        pe.wait_ge(sines, i * (5 * UNITS * BODY) + (after[(uu, s)] + SC))

                    def magic_step(s):
                        slot_free(s)
                        angles(w, uu, s, True, True, True)
                        angles(w, uu, s, True, False, False)
                        angles(w, uu, s, False, True, False)
                        angles(w, uu, s, False, False, False).then_inc(angle_ready, 1)

                    slot_free(V0)
                    angles(w, uu, V0, False, False, True).then_inc(raw_ready, 1)
                    magic_step(P1)
                    pe.wait_ge(turns_ready, U * 2 + 1)
                    less_turns(uu, V0, 0).then_inc(angle_ready, 1)
                    magic_step(P3)
                    slot_free(V2)
                    angles(w, uu, V2, False, False, True).then_inc(raw_ready, 1)
                    magic_step(P4)
                    pe.wait_ge(turns_ready, U * 2 + 2)
                    less_turns(uu, V2, 1).then_inc(angle_ready, 1)
                    prev = (uu - 1) % (UNITS * BODY)
                    n_prev = i * BODY + (-1 if uu == 0 else (uu - 1) // UNITS)
                    pv_product(pe, prev // UNITS, prev, U, n_prev, uu % UNITS == UNITS - 1)
            last_u = UNITS * BODY - 1
            pv_product(pe, BODY - 1, last_u, NBH * UNITS, NBH - 1)

        @block.scalar
        def _(act):
            act.wait_ge(cleared, CLEAR)

            def tanh(uu, U):
                act.wait_ge(sums, U * SUMS + (AC - 1))
                act.wait_ge(products, U + (VC - 3))
                nc.scalar.activation(wt[:, uu % 2, :, :], acc[:, uu % 2, :, :], ACT.Tanh, scale=0.5).then_inc(tanhs, 1)

            def evacuate(w, n, i):
                act.wait_ge(products, n * UNITS + (VC - 1))
                act.wait_ge(stored[w], i * 64 + 16)
                nc.scalar.activation(obuf[:, w, :], pv[:], ACT.Copy).then_inc(evacs, 1)

            def store(w, n):
                act.wait_ge(evacs, n + 1)
                for k in range(4):
                    act.dma_start(g.NUM[n, k], obuf[32 * k:32 * k + HD0 + 1, w, :]).then_inc(stored[w], 16)

            nc.scalar.activation(credit[:, 8:9], credit[:, 9:10], ACT.Silu).then_inc(silu_loaded, 1)
            with act.Fori(0, NBH // BODY) as i:
                for uu in range(UNITS * BODY):
                    U = i * (UNITS * BODY) + uu
                    if uu % UNITS == 1:
                        evacuate((uu // UNITS - 1) % BODY, i * BODY + uu // UNITS, i)
                    for a, s in enumerate(SIN_ORDER):
                        act.wait_ge(angle_ready, U * 5 + (a + 1))
                        if a == 0:
                            act.wait_ge(firsts, U + (FC - 1))
                        else:
                            act.wait_ge(sums, U * SUMS + (a - 1 - SUMS + AC))
                        nc.scalar.activation(wave[:, a, :, :], ps[:, slot[(uu, s)], :, :], ACT.Sin,
                                             scale=TURN).then_inc(sines, 1)
                        if a == 1:
                            tanh((uu - 1) % 2, U)
                    if uu % UNITS == 3:
                        store((uu // UNITS - 1) % BODY, i * BODY + uu // UNITS)
            tanh(1, NBH * UNITS)
            evacuate(BODY - 1, NBH, NBH // BODY)
            store(BODY - 1, NBH)
            act.wait_ge(stored[0], 16 + 64 * (NBH // 2))
            act.wait_ge(stored[1], 16 + 64 * (NBH // 2 + 1))

        @block.vector
        def _(v):
            v.memset(turns[:], 0.0).then_inc(cleared, 1)
            v.memset(credit[:, 9:10], 0.0).then_inc(cleared, 1)
            v.memset(wave[:], 0.0).then_inc(cleared, 1)
            v.memset(acc[:], 0.0).then_inc(cleared, 1)
            v.memset(wt[:], 0.0).then_inc(cleared, 1)
            nc.vector.tensor_scalar(negi[:], g.ident[:], -1.0, None, ALU.mult).then_inc(cleared, 1)
            for k, (done, count) in enumerate(((stack_used, BODY), (sines, SC - 1), (firsts, FC - 1), (sums, AC - 3), (tanhs, TC - 2),
                                               (products, VC - 2), (stored[0], 16), (stored[1], 16))):
                v.memset(credit[:, k:k + 1], 0.0).then_inc(done, count)
            v.wait_ge(cleared, CLEAR)
            v.wait_ge(pv_cleared, 1)

            def whole_turns(uu, s, U, k):
                v.wait_ge(raw_ready, U * 2 + (k + 1))
                nc.vector.tensor_scalar(turns[:, k, :, :], ps[:, slot[(uu, s)], :, :], MAGIC, -MAGIC, ALU.add,
                                        ALU.add).then_inc(turns_ready, 1)

            def add_wave(uu, a, U, back):
                w, s = uu // UNITS, SIN_ORDER[a]
                v.wait_ge(sines, U * NF + (a + SC - NF * back))
                if a == 1:
                    v.wait_ge(firsts, U + FC)
                v.wait_ge(sums, U * SUMS + (a - 2 + AC - SUMS * back))
                total = acc[:, uu % 2, :, :]
                nc.vector.scalar_tensor_tensor(out=total, in0=wave[:, a, :, :], scalar=acur[:, w, s:s + 1], in1=total,
                                               op0=ALU.mult, op1=ALU.add).then_inc(sums, 1)

            with v.Fori(0, NBH // BODY) as i:
                for uu in range(UNITS * BODY):
                    w, U = uu // UNITS, i * (UNITS * BODY) + uu
                    before = (uu - 1) % (UNITS * BODY)
                    whole_turns(uu, V0, U, 0)
                    add_wave(before, 3, U, 1)
                    add_wave(before, 4, U, 1)
                    whole_turns(uu, V2, U, 1)
                    if uu % UNITS == 0:
                        v.wait_ge(alpha_ready, i * BODY + (w + 1))
                    add_wave(uu, 1, U, 0)
                    add_wave(uu, 2, U, 0)
            for a in (3, 4):
                add_wave(UNITS * BODY - 1, a, NBH * UNITS, 1)


def stage_out0(nc, g):
    with ExitStack() as ctx:
        def sb(n, s, dt=F32):
            return ctx.enter_context(nc.sbuf_tensor(n, s, dt))
        num = sb("num", [P, 2, 2, QB])
        den = sb("den", [H0, 2, 2, QB])
        rden = sb("rden", [H0, 3, QB])
        tot = sb("tot", [P, 2, QB])
        aT = sb("aT", [P, 2, QB])
        wo, bo, sel = sb("wo", [P, D]), sb("bo", [1, D]), sb("sel", [H0, P])
        o = sb("o", [P, NT, D])
        st, mv, sd = sb("ost", [P, NT, 6]), sb("omv", [P, NT, 2]), sb("osd", [P, 3, NT])
        psb = ctx.enter_context(nc.psum_tensor("psb", [P, 2, QB], F32))
        pso = ctx.enter_context(nc.psum_tensor("pso", [P, 2, 4, D], F32))
        names = ("ow_in", "den1", "den2", "den3", "tot1", "bcast", "aT_done", "o_mm", "o_copied", "ostats",
                 "oaggr", "oveps", "oroot", "orinv", "onorm", "oscaled", "oadd")
        (w_in, den1, den2, den3, tot1, bcast, aT_done, o_mm, o_copied, stats, aggr, veps, root, rinv,
         onorm, oscaled, oadd) = sems(nc, g, *names)
        num_in = two(nc, g, "num_in")
        block = ctx.enter_context(nc.Block())

        @block.sync
        def _(sp):
            for dst, src in ((wo[:], g.src["wo0"]), (bo[:], g.src["bo0"]), (sel[:], g.src["k_sel"])):
                sp.dma_start(dst, src).then_inc(w_in, 16)
            for c in range(NC):
                b, qh = c // 2, c % 2
                rows = g.NUM[1 + H0 * b:1 + H0 * (b + 1)]
                if c >= 2:
                    sp.wait_ge(tot1, c - 1)
                    sp.wait_ge(den1, c - 1)
                for a in range(2):
                    sp.dma_start(num[:, c % 2, a, :],
                                 rows[:, 2 * qh + a, 0:HD0, :]).then_inc(num_in[c % 2], 16)
                    sp.dma_start(den[:, c % 2, a, :], rows[:, 2 * qh + a, HD0, :]).then_inc(num_in[c % 2], 16)

        @block.tensor
        def _(pe):
            pe.wait_ge(w_in, 48)
            for c in range(NC):
                pe.wait_ge(den3, c + 1)
                if c >= 2:
                    pe.wait_ge(aT_done, c - 1)
                nc.tensor.matmul(psb[:, c % 2, :], sel[:], rden[:, 2, :], start=True, stop=True).then_inc(bcast, 1)
                pe.wait_ge(aT_done, c + 1)
                if c >= 2:
                    pe.wait_ge(o_copied, c - 1)
                for k in range(4):
                    nc.tensor.matmul(pso[:, c % 2, k, :], aT[:, c % 2, P * k:P * (k + 1)], wo[:], start=True, stop=False)
                    last = nc.tensor.matmul(pso[:, c % 2, k, :], g.ones[0:1, :], bo[:], start=False, stop=True)
                last.then_inc(o_mm, 1)

        @block.scalar
        def _(act):
            for c in range(NC):
                act.wait_ge(o_mm, c + 1)
                nc.scalar.activation(o[:, 4 * c:4 * c + 4, :], pso[:, c % 2, :, :], ACT.Copy).then_inc(o_copied, 1)
            act.wait_ge(veps, 1)
            nc.scalar.activation(sd[:, 1, :], sd[:, 0, :], ACT.Sqrt).then_inc(root, 1)

        @block.vector
        def _(v):
            for c in range(NC):
                b = c // 2
                v.wait_ge(num_in[c % 2], 64 * (c // 2 + 1))
                if c >= 1:
                    v.wait_ge(bcast, c)
                nc.vector.scalar_tensor_tensor(out=rden[:, 0, :], in0=den[:, c % 2, 0, :], scalar=float(L),
                                               in1=den[:, c % 2, 1, :], op0=ALU.add, op1=ALU.add).then_inc(den1, 1)
                v.wait_ge(den1, c + 1)
                nc.vector.tensor_scalar(rden[:, 1, :], rden[:, 0, :], 2e-10, None, ALU.add).then_inc(den2, 1)
                v.wait_ge(den2, c + 1)
                nc.vector.reciprocal(rden[:, 2, :], rden[:, 1, :]).then_inc(den3, 1)
                nc.vector.scalar_tensor_tensor(out=tot[:, c % 2, :], in0=num[:, c % 2, 0, :], scalar=g.vsum[:, b:b + 1],
                                               in1=num[:, c % 2, 1, :], op0=ALU.add, op1=ALU.add).then_inc(tot1, 1)
                v.wait_ge(tot1, c + 1)
                v.wait_ge(bcast, c + 1)
                if c >= 2:
                    v.wait_ge(o_mm, c - 1)
                nc.vector.tensor_tensor(aT[:, c % 2, :], tot[:, c % 2, :], psb[:, c % 2, :], ALU.mult).then_inc(aT_done, 1)
            for t in range(NT):
                v.wait_ge(o_copied, t // 4 + 1)
                nc.vector.bn_stats(st[:, t, :], o[:, t, :]).then_inc(stats, 1)
            for t in range(NT):
                v.wait_ge(stats, t + 1)
                nc.vector.bn_aggr(mv[:, t, :], st[:, t, :]).then_inc(aggr, 1)
            v.wait_ge(aggr, NT)
            nc.vector.tensor_scalar(sd[:, 0, :], mv[:, :, 1], EPS, None, ALU.add).then_inc(veps, 1)
            v.wait_ge(root, 1)
            nc.vector.reciprocal(sd[:, 2, :], sd[:, 1, :]).then_inc(rinv, 1)
            v.wait_ge(rinv, 1)
            for b in range(B):
                for t in range(TB * b, TB * (b + 1)):
                    nc.vector.tensor_scalar(o[:, t, :], o[:, t, :], mv[:, t, 0:1], sd[:, 2, t:t + 1],
                                            ALU.subtract, ALU.mult).then_inc(onorm, 1)
                ob, xb = o[:, TB * b:TB * (b + 1), :], g.x[:, TB * b:TB * (b + 1), :]
                v.wait_ge(onorm, TB * (b + 1))
                nc.vector.tensor_tensor(ob, ob, g.bc[:, 0, b:b + 1, :].to_broadcast([P, TB, D]), ALU.mult).then_inc(oscaled, 1)
                v.wait_ge(oscaled, 2 * b + 1)
                nc.vector.tensor_tensor(ob, ob, g.bc[:, 1, b:b + 1, :].to_broadcast([P, TB, D]), ALU.add).then_inc(oscaled, 1)
                v.wait_ge(oscaled, 2 * b + 2)
                nc.vector.tensor_tensor(xb, xb, ob, ALU.add).then_inc(oadd, 1)
            v.wait_ge(oadd, B)


def stage_route0(nc, g):
    with ExitStack() as ctx:
        def sb(n, s, dt=F32):
            return ctx.enter_context(nc.sbuf_tensor(n, s, dt))
        wg, bg = sb("wg", [P, E0]), sb("bg", [1, E0])
        iot, tokid = sb("iot", [P, E0]), sb("tokid", [P, NT])
        tri, one = sb("tri", [P, P], BF16), sb("oneb", [P, P], BF16)
        lg, cand, ex, full = sb("lg", [P, NT, E0]), sb("cand", [P, NT, E0]), sb("ex", [P, NT, E0]), sb("full", [P, NT, E0])
        oneh = sb("oneh", [P, NT, E0], BF16)
        scan = sb("scan", [P, 2, NT, E0])
        col = sb("rcol", [P, 10, NT])
        zero = sb("zero", [P, 2048])
        psl = ctx.enter_context(nc.psum_tensor("psl", [P, NT, E0], F32))
        psp = ctx.enter_context(nc.psum_tensor("psp", [P, 2, NT, E0], F32))
        names = ("rw_in", "zeroed", "zero_out", "logits", "rstep", "exped", "counts", "low_done", "rows_out")
        w_in, zeroed, zero_out, logits, rstep, exped, counts, low_done, rows_out = sems(nc, g, *names)
        loads = [(wg[:], g.src["wg0"]), (bg[:], g.src["bg0"]), (iot[:], g.src["k_iota"]), (tokid[:], g.src["k_tok"]), (tri[:], g.src["k_tri"]), (one[:], g.src["k_one"])]
        block = ctx.enter_context(nc.Block())
        index_ready = [None]

        @block.sync
        def _(sp):
            for dst, src in loads:
                sp.dma_start(dst, src).then_inc(w_in, 16)
            sp.wait_ge(zeroed, 1)
            for k in range(2):
                sp.dma_start(g.ROWS[E0 * CAP // 2 * k:E0 * CAP // 2 * (k + 1), :].rearrange("(p r) d -> p (r d)", p=P),
                             zero[:]).then_inc(zero_out, 16)

        @block.tensor
        def _(pe):
            pe.wait_ge(w_in, 16 * len(loads))
            for t in range(NT):
                nc.tensor.matmul(psl[:, t, :], g.hT[:, P * t:P * (t + 1)], wg[:], start=True, stop=False)
                last = nc.tensor.matmul(psl[:, t, :], g.ones[0:1, :], bg[:], start=False, stop=True)
            last.then_inc(logits, 1)
            pe.wait_ge(rstep, 6)
            hot = oneh[:].rearrange("p t e -> p (t e)")
            nc.tensor.matmul(psp[:, 0].rearrange("p t e -> p (t e)"), tri[:], hot, start=True, stop=True)
            nc.tensor.matmul(psp[:, 1].rearrange("p t e -> p (t e)"), one[:], hot, start=True, stop=True).then_inc(counts, 1)

        @block.scalar
        def _(act):
            act.wait_ge(rstep, 3)
            nc.scalar.activation(ex[:], ex[:], ACT.Exp).then_inc(exped, 1)

        @block.vector
        def _(v):
            n = [0]
            nc.vector.memset(zero[:], 0.0).then_inc(zeroed, 1)
            v.wait_ge(w_in, 16 * len(loads))
            v.wait_ge(logits, 1)

            def done(ins):
                n[0] += 1
                ins.then_inc(rstep, 1)
                v.wait_ge(rstep, n[0])

            def wide(c):
                return c.rearrange("p (t o) -> p t o", o=1).to_broadcast([P, NT, E0])

            iob = iot[:].rearrange("p (o e) -> p o e", o=1).to_broadcast([P, NT, E0])
            top, low, eid, pos, keep, gate, posc, gi, si, den = [col[:, k, :] for k in range(10)]
            done(nc.vector.tensor_copy(lg[:], psl[:]))
            done(nc.vector.tensor_reduce(top, lg[:], AX.X, ALU.max))
            done(nc.vector.tensor_tensor(ex[:], lg[:], wide(top), ALU.subtract))
            done(nc.vector.tensor_tensor(cand[:], lg[:], wide(top), ALU.is_equal))
            done(nc.vector.scalar_tensor_tensor(out=full[:], in0=cand[:], scalar=-float(E0), in1=iob, op0=ALU.mult, op1=ALU.add))
            nc.vector.tensor_reduce(low, full[:], AX.X, ALU.min).then_inc(low_done, 1)
            v.wait_ge(low_done, 1)
            nc.vector.tensor_scalar(eid, low, float(E0), None, ALU.add).then_inc(low_done, 1)
            v.wait_ge(low_done, 2)
            done(nc.vector.tensor_tensor(oneh[:], iob, wide(eid), ALU.is_equal))
            v.wait_ge(exped, 1)
            done(nc.vector.tensor_reduce(den, ex[:], AX.X, ALU.add))
            done(nc.vector.reciprocal(gate, den))
            v.wait_ge(counts, 1)
            done(nc.vector.tensor_copy(scan[:, 0], psp[:, 1]))
            k = 0
            for s in (1, 2, 4, 8, 16):
                nc.vector.tensor_copy(scan[:, 1 - k, 0:s], scan[:, k, 0:s])
                done(nc.vector.tensor_tensor(scan[:, 1 - k, s:], scan[:, k, s:], scan[:, k, 0:NT - s], ALU.add))
                k = 1 - k
            nc.vector.tensor_copy(full[:, 0:1, :], psp[:, 0, 0:1, :])
            done(nc.vector.tensor_tensor(full[:, 1:, :], psp[:, 0, 1:, :], scan[:, k, 0:NT - 1, :], ALU.add))
            done(nc.vector.tensor_tensor(cand[:], full[:], oneh[:], ALU.mult))
            done(nc.vector.tensor_reduce(pos, cand[:], AX.X, ALU.add))
            done(nc.vector.tensor_scalar(keep, pos, float(CAP), None, ALU.is_lt))
            done(nc.vector.tensor_scalar(posc, pos, float(CAP - 1), None, ALU.min))
            done(nc.vector.scalar_tensor_tensor(out=gi, in0=eid, scalar=float(CAP), in1=posc, op0=ALU.mult, op1=ALU.add))
            done(nc.vector.tensor_copy(g.gidx[:], gi))
            done(nc.vector.tensor_tensor(si, gi, tokid[:], ALU.subtract))
            done(nc.vector.tensor_tensor(low, si, keep, ALU.mult))
            done(nc.vector.tensor_tensor(si, low, tokid[:], ALU.add))
            done(nc.vector.tensor_tensor(g.gate[:], gate, keep, ALU.mult))
            done(nc.vector.tensor_copy(g.sidx[:], si))
            index_ready[0] = n[0]

        @block.gpsimd
        def _(pool):
            pool.wait_ge(zero_out, 32)
            pool.wait_ge(rstep, index_ready[0])
            for t in range(NT):
                pool.indirect_dma_start(g.ROWS, bass.IndirectOffsetOnAxis(ap=g.sidx[:, t:t + 1], axis=0), g.h[:, t, :],
                                        None).then_inc(rows_out, 16)
            pool.wait_ge(rows_out, 16 * NT)


def stage_experts0(nc, g):
    NB = CAP // P
    NK = HF // P
    NW = 4
    with ExitStack() as ctx:
        def sb(n, s, dt=F32):
            return ctx.enter_context(nc.sbuf_tensor(n, s, dt))
        rows, rowsT = sb("rows", [P, NW, NB, D]), sb("rowsT", [P, 2, CAP])
        w1, w2, b2 = sb("w1", [P, NW, HF]), sb("w2", [P, NW, NK, D]), sb("b2", [1, NW, D])
        b1 = sb("b1", [P, E0, NK])
        hid, y = sb("hid", [P, 2, NK, CAP]), sb("y", [P, 2, NB, D])
        ps_t = ctx.enter_context(nc.psum_tensor("ps_t", [P, 2, 512], F32))
        ps_h = ctx.enter_context(nc.psum_tensor("ps_h", [P, 2, NK, CAP], F32))
        ps_y = ctx.enter_context(nc.psum_tensor("ps_y", [P, 2, 512], F32))
        b1_in, turned, rows_moved, hid_mm, hid_done, y_mm, y_moved, started = sems(
            nc, g, "b1_in", "turned", "rows_moved", "hid_mm", "hid_done", "y_mm", "y_moved", "started")
        expert_in, y_out = sems(nc, g, *["expert_in%d" % w for w in range(NW)]), two(nc, g, "y_out")
        block = ctx.enter_context(nc.Block())
        W1, W2, B2 = g.src["w1"], g.src["w2"], g.src["b2"]
        ROWS = g.ROWS[0:E0 * CAP].rearrange("(e k p) d -> e p k d", e=E0, p=P)
        YR = g.Y.rearrange("(e k p) d -> e p k d", e=E0, p=P)

        @block.sync
        def _(sp):
            sp.dma_start(b1[:], g.src["b1"]).then_inc(b1_in, 16)
            with sp.Fori(0, E0 // NW) as i:
                for w in range(NW):
                    e = i * NW + w
                    sp.wait_ge(y_mm, e + 1)
                    sp.dma_start(rows[:, w, :, :], ROWS[e]).then_inc(expert_in[w], 16)
                    sp.dma_start(w1[:, w, :], W1[e]).then_inc(expert_in[w], 16)
                    sp.dma_start(w2[:, w, :, :], W2[e]).then_inc(expert_in[w], 16)
                    sp.dma_start(b2[:, w, :], B2[e]).then_inc(expert_in[w], 16)

        @block.tensor
        def _(pe):
            def first(i, w):
                e = i * NW + w
                pe.wait_ge(expert_in[w], i * 64 + 64)
                for k in range(NB):
                    last = nc.tensor.transpose(ps_t[:, w % 2, P * k:P * (k + 1)], rows[:, w, k, :], g.ident[:])
                last.then_inc(turned, 1)
                pe.wait_ge(rows_moved, e + 1)
                pe.wait_ge(hid_done, e + 1)
                for c in range(NK):
                    last = nc.tensor.matmul(ps_h[:, w % 2, c, :], w1[:, w, P * c:P * (c + 1)], rowsT[:, w % 2, :],
                                            start=True, stop=True)
                last.then_inc(hid_mm, 1)

            def second(i, w):
                pe.wait_ge(hid_done, i * NW + (w + 3))
                for k in range(NB):
                    y_k = ps_y[:, w % 2, D * k:D * (k + 1)]
                    for c in range(NK):
                        nc.tensor.matmul(y_k, hid[:, w % 2, c, P * k:P * (k + 1)], w2[:, w, c, :], start=(c == 0), stop=False)
                    last = nc.tensor.matmul(y_k, g.ones[0:1, :], b2[:, w, :], start=False, stop=True)
                last.then_inc(y_mm, 1)

            pe.wait_ge(started, 1)
            with pe.Fori(0, E0 // NW) as i:
                first(i, 0)
                for w in range(1, NW):
                    first(i, w)
                    second(i, w - 1)
                second(i, NW - 1)

        @block.scalar
        def _(act):
            def move_rows(i, w):
                act.wait_ge(turned, i * NW + (w + 1))
                nc.scalar.activation(rowsT[:, w % 2, :], ps_t[:, w % 2, 0:CAP], ACT.Copy).then_inc(rows_moved, 1)

            def store(i, w):
                e = i * NW + w
                act.wait_ge(y_mm, e + (NW + 1))
                act.wait_ge(y_out[w % 2], i * (8 * NW) + (16 * (w // 2) + 16))
                nc.scalar.activation(y[:, w % 2, :, :], ps_y[:, w % 2, 0:NB * D].rearrange("p (k d) -> p k d", k=NB),
                                     ACT.Copy).then_inc(y_moved, 1)
                act.wait_ge(y_moved, e + 1)
                act.dma_start(YR[e], y[:, w % 2, :, :]).then_inc(y_out[w % 2], 16)

            act.wait_ge(started, 1)
            with act.Fori(0, E0 // NW) as i:
                move_rows(i, 0)
                for w in range(1, NW):
                    move_rows(i, w)
                    store(i, w - 1)
                store(i, NW - 1)
            for w in range(2):
                act.wait_ge(y_out[w], 16 * (E0 // 2 + 1))

        @block.vector
        def _(v):
            v.memset(hid[:, 0, 0, 0:1], 0.0).then_inc(y_mm, NW)
            v.memset(hid[:, 0, 1, 0:1], 0.0).then_inc(hid_done, 2)
            for w in range(2):
                v.memset(hid[:, 1, w, 0:1], 0.0).then_inc(y_out[w], 16)
            v.memset(hid[:, 0, 2, 0:1], 0.0).then_inc(started, 1)
            v.wait_ge(started, 1)
            v.wait_ge(b1_in, 16)
            with v.Fori(0, E0 // NW) as i:
                for w in range(NW):
                    e = i * NW + w
                    v.wait_ge(hid_mm, e + 1)
                    for c in range(NK):
                        ins = nc.vector.tensor_scalar(hid[:, w % 2, c, :], ps_h[:, w % 2, c, :], b1[:, bass.ds(e, 1), c],
                                                      0.0, ALU.add, ALU.max)
                    ins.then_inc(hid_done, 1)


def stage_combine0(nc, g):
    with ExitStack() as ctx:
        yg = ctx.enter_context(nc.sbuf_tensor("yg", [P, NT, D], F32))
        gated, scaled, added = sems(nc, g, "gated", "scaled", "added")
        gathered = sems(nc, g, *["gathered%d" % b for b in range(B)])
        block = ctx.enter_context(nc.Block())

        @block.gpsimd
        def _(pool):
            for t in range(NT):
                pool.indirect_dma_start(yg[:, t, :], None, g.Y, bass.IndirectOffsetOnAxis(ap=g.gidx[:, t:t + 1], axis=0)
                                        ).then_inc(gathered[t // TB], 16)

        @block.vector
        def _(v):
            for b in range(B):
                v.wait_ge(gathered[b], 16 * TB)
                for t in range(TB * b, TB * (b + 1)):
                    nc.vector.tensor_scalar(yg[:, t, :], yg[:, t, :], g.gate[:, t:t + 1], None, ALU.mult).then_inc(gated, 1)
                yb, xb = yg[:, TB * b:TB * (b + 1), :], g.x[:, TB * b:TB * (b + 1), :]
                v.wait_ge(gated, TB * (b + 1))
                nc.vector.tensor_tensor(yb, yb, g.bc[:, 4, b:b + 1, :].to_broadcast([P, TB, D]), ALU.mult).then_inc(scaled, 1)
                v.wait_ge(scaled, b + 1)
                nc.vector.tensor_tensor(xb, xb, yb, ALU.add).then_inc(added, 1)
            v.wait_ge(added, B)


def stage_attention1(nc, g):
    STEPS = B * TB * 2
    LAG_T, LAG_V = 2, 4
    NP, NTURN = 5, 3

    def step(t):
        b, q = t // 16, t % 16 // 2
        return b, (q if b % 2 == 0 else TB - 1 - q), t % 2

    def half_of(n):
        return n % 2 if n // 2 % 2 == 0 else 1 - n % 2

    side = []
    for t in range(STEPS + LAG_V):
        b, r = t // 16, t % 16
        if 4 <= r < 12 and b < B:
            side.append((t, "proj", b + 1, r - 4))
        if b > 0 and r in (13, 14) and b < B:
            side.append((t, "wo", b - 1, r - 13))
    side += [(STEPS + LAG_V, "wo", B - 1, k) for k in range(2)]
    NS = len(side)

    with ExitStack() as ctx:
        def sb(n, s, dt=F32):
            return ctx.enter_context(nc.sbuf_tensor(n, s, dt))
        wqkv, wo = sb("wqkv", [P, 3, P]), sb("wo1", [P, D])
        qz = sb("qz", [P, 2, 2, L])
        kv = sb("kv", [P, 2, 2, L])
        vt = sb("vt", [P, 2, TB, P])
        pr = sb("pr", [P, NP, L])
        pT = sb("pT", [P, NTURN, TB, P])
        mx, nb, rs, ri = sb("mx", [P, NP]), sb("nb", [P, NP]), sb("rs", [P, NP]), sb("ri", [P, NP])
        cT = sb("cT", [P, 2, 2, QB])
        yT = sb("yT", [P, T])
        idb, mask = sb("idb", [P, P], BF16), sb("mask", [P, P], BF16)
        ps_s = ctx.enter_context(nc.psum_tensor("ps_s", [P, 2, L], F32))
        ps_t = ctx.enter_context(nc.psum_tensor("ps_t1", [P, TB, P], F32))
        ps_o = ctx.enter_context(nc.psum_tensor("ps_o", [P, QB], F32))
        ps_e = ctx.enter_context(nc.psum_tensor("ps_side", [P, QB], F32))
        (const_in, wqkv_in, wo_in, q_clear, y_clear, side_mm, side_done, score_mm, maxed, shift, exped, inverse, normed, turned, moved,
         products, taken, scaled, turned_y, added) = sems(
            nc, g, "a_const_in", "a_wqkv_in", "a_wo_in", "q_clear", "y_clear", "side_mm", "side_done", "score_mm", "maxed", "shift", "a_exped",
            "inverse", "normed", "a_turned", "a_moved", "a_products", "taken", "a_scaled", "turned_y", "a_added")
        block = ctx.enter_context(nc.Block())
        proj_uses = [n for n, s_ in enumerate(side) if s_[1] == "proj"]
        PRE = 8
        last_own = proj_uses[8 * (B - 1) - 1]

        def move(eng, seq, i, u):
            b, q, hh = step(u)
            seq.wait_ge(turned, i * STEPS + (u + 1))
            if u >= NTURN:
                seq.wait_ge(products, i * STEPS + (u - NTURN + 1))
            dst, src = pT[:, u % NTURN, 0:q + 1, :], ps_t[:, 0:q + 1, :]
            if u % 2 == 0:
                nc.scalar.activation(dst, src, ACT.Copy).then_inc(moved, 1)
            else:
                nc.vector.tensor_copy(dst, src).then_inc(moved, 1)

        @block.sync
        def _(sp):
            sp.dma_start(idb[:], g.src["k_identb"]).then_inc(const_in, 16)
            sp.dma_start(mask[:], g.src["k_mask"]).then_inc(const_in, 16)
            sp.dma_start(wqkv[:], g.src["wqkv1"][0]).then_inc(wqkv_in, 16)
            with sp.Fori(0, HP) as i:
                sp.wait_ge(side_mm, i * NS + (PRE + 1))
                sp.dma_start(wo[:], g.src["wo1"][i]).then_inc(wo_in, 16)
                sp.wait_ge(side_mm, i * NS + (PRE + last_own + 2))
                sp.dma_start(wqkv[:], g.src["wqkv1"][i + 1]).then_inc(wqkv_in, 16)

        @block.tensor
        def _(pe):
            pe.wait_ge(const_in, 32)

            def project(b, k):
                if k < 6:
                    c = L * (b % B) + QB * (k % 2)
                    return nc.tensor.matmul(ps_e[:], wqkv[:, k // 2, :], g.hT[:, c:c + QB], start=True, stop=True)
                for j in range(4):
                    c = QB * (k - 6) + P * j
                    last = nc.tensor.transpose(ps_e[:, P * j:P * (j + 1)], kv[:, b % 2, 1, c:c + P], g.ident[:])
                return last

            def side_use(i, n):
                _, kind, b, k = side[n]
                pe.wait_ge(side_done, i * NS + (PRE + n + 1))
                if kind == "wo":
                    if b == 0 and k == 0:
                        pe.wait_ge(wo_in, i * 16 + 16)
                    pe.wait_ge(taken, i * (2 * B) + (2 * b + half_of(2 * b + k) + 2))
                    last = nc.tensor.matmul(ps_e[:], wo[:], cT[:, b % 2, k, :], start=True, stop=True)
                else:
                    if b == B and k == 0:
                        pe.wait_ge(wqkv_in, i * 16 + 32)
                    last = project(b, k)
                last.then_inc(side_mm, 1)

            def scores(i, t):
                b, q, hh = step(t)
                if t % 16 == 0:
                    pe.wait_ge(side_done, i * NS + (PRE + 1 if b == 0 else PRE + proj_uses[8 * b - 1] + 2))
                if t >= 2:
                    pe.wait_ge(exped, i * STEPS + (t - 1))
                W = P * (q + 1)
                lhs = qz[:, b % 2, hh, P * q:P * (q + 1)]
                for c in range(0, W, QB):
                    hi = min(W, c + QB)
                    end = hi == W
                    last = nc.tensor.matmul(ps_s[:, t % 2, c:hi], lhs, kv[:, b % 2, 0, c:hi], start=True,
                                            stop=not end, skip_group_check=True)
                last = nc.tensor.matmul(ps_s[:, t % 2, W - P:W], idb[:], mask[:], start=False, stop=True,
                                        skip_group_check=True)
                last.then_inc(score_mm, 1)

            def turn(i, t):
                b, q, hh = step(t)
                pe.wait_ge(normed, i * STEPS + (t + 1))
                if t >= 1:
                    pe.wait_ge(moved, i * STEPS + t)
                for j in range(q + 1):
                    last = nc.tensor.transpose(ps_t[:, j, :], pr[:, t % NP, P * j:P * (j + 1)], g.ident[:])
                last.then_inc(turned, 1)

            def value(i, t):
                b, q, hh = step(t)
                pe.wait_ge(moved, i * STEPS + (t + 1))
                if t % 8 == 0:
                    pe.wait_ge(taken, i * (2 * B) + (t // 8 + 1))
                r = 64 * hh
                for j in range(q + 1):
                    last = nc.tensor.matmul(ps_o[r:r + HD1, P * (q % 4):P * (q % 4 + 1)], vt[:, b % 2, j, r:r + HD1],
                                            pT[:, t % NTURN, j, :], start=(j == 0), stop=(j == q), skip_group_check=True)
                last.then_inc(products, 1)

            pe.wait_ge(wqkv_in, 16)
            for k in range(PRE):
                pe.wait_ge(side_done, k + 1)
                project(0, k).then_inc(side_mm, 1)
            with pe.Fori(0, HP) as i:
                for t in range(STEPS + LAG_V):
                    if t < STEPS:
                        scores(i, t)
                    if LAG_T <= t < STEPS + LAG_T:
                        turn(i, t - LAG_T)
                    if t >= LAG_V:
                        value(i, t - LAG_V)
                    for n in range(NS):
                        if side[n][0] == t:
                            side_use(i, n)
                for n in range(NS - 2, NS):
                    side_use(i, n)
            for c in range(NC):
                pe.wait_ge(scaled, c + 1)
                if c >= 1:
                    pe.wait_ge(added, c)
                for k in range(4):
                    last = nc.tensor.transpose(ps_e[:, P * k:P * (k + 1)], yT[:, QB * c + P * k:QB * c + P * (k + 1)], g.ident[:])
                last.then_inc(turned_y, 1)

        @block.scalar
        def _(act):
            def take_projection(b, k):
                c = QB * (k % 2)
                if k < 2:
                    nc.scalar.activation(qz[0:HD1, b % 2, 0, c:c + QB], ps_e[0:HD1, :], ACT.Copy)
                    return nc.scalar.activation(qz[HD1:P, b % 2, 1, c:c + QB], ps_e[HD1:P, :], ACT.Copy)
                if k < 6:
                    return nc.scalar.activation(kv[:, b % 2, k // 2 - 1, c:c + QB], ps_e[:], ACT.Copy)
                dst = vt[:, b % 2, 4 * (k - 6):4 * (k - 5), :].rearrange("p t d -> p (t d)")
                return nc.scalar.activation(dst, ps_e[:], ACT.Copy)

            act.wait_ge(q_clear, 1)
            for k in range(PRE):
                act.wait_ge(side_mm, k + 2)
                take_projection(0, k).then_inc(side_done, 1)
            with act.Fori(0, HP) as i:
                for t in range(STEPS + LAG_V):
                    if t < STEPS:
                        b, q, hh = step(t)
                        W = P * (q + 1)
                        act.wait_ge(shift, i * STEPS + (t + 1))
                        if t >= NP:
                            act.wait_ge(turned, i * STEPS + (t - NP + 1))
                        nc.scalar.activation(pr[:, t % NP, 0:W], ps_s[:, t % 2, 0:W], ACT.Exp, bias=nb[:, t % NP:t % NP + 1],
                                             scale=float(HD1) ** -0.5, accum_out=rs[:, t % NP:t % NP + 1]).then_inc(exped, 1)
                    u = t - LAG_T
                    if 0 <= u < STEPS and u % 2 == 0:
                        move(nc.scalar, act, i, u)
                    for n in range(NS):
                        if side[n][0] == t and side[n][1] == "proj":
                            act.wait_ge(side_mm, i * NS + (PRE + n + 2))
                            take_projection(side[n][2], side[n][3]).then_inc(side_done, 1)

        @block.gpsimd
        def _(pool):
            nc.gpsimd.memset(qz[:], 0.0).then_inc(q_clear, 1)
            with pool.Fori(0, HP) as i:
                for t in range(STEPS):
                    b, q, hh = step(t)
                    pool.wait_ge(inverse, i * STEPS + (t + 1))
                    W = P * (q + 1)
                    nc.gpsimd.tensor_tensor(pr[:, t % NP, 0:W], pr[:, t % NP, 0:W],
                                            ri[:, t % NP:t % NP + 1].to_broadcast([P, W]), ALU.mult).then_inc(normed, 1)

        @block.vector
        def _(v):
            nc.vector.memset(yT[:], 0.0).then_inc(y_clear, 1)
            for k, count in enumerate((side_mm, side_done, taken)):
                nc.vector.memset(mx[:, k:k + 1], 0.0).then_inc(count, 1)
            v.wait_ge(y_clear, 1)

            def take(i, half):
                v.wait_ge(products, i * STEPS + 8 * (half + 1))
                b, k = half // 2, half_of(half)
                if b >= 2:
                    n = [m for m, s_ in enumerate(side) if s_[1:] == ("wo", b - 2, k)][0]
                    v.wait_ge(side_mm, i * NS + (PRE + n + 2))
                nc.vector.tensor_copy(cT[:, b % 2, k, :], ps_o[:]).then_inc(taken, 1)

            def add_wo(i, n):
                _, _, b, k = side[n]
                v.wait_ge(side_mm, i * NS + (PRE + n + 2))
                dst = yT[:, L * b + QB * k:L * b + QB * (k + 1)]
                nc.vector.tensor_tensor(dst, ps_e[:], dst, ALU.add).then_inc(side_done, 1)

            with v.Fori(0, HP) as i:
                for t in range(STEPS + LAG_V + 1):
                    if t >= LAG_V + 8 and (t - LAG_V) % 8 == 0:
                        take(i, (t - LAG_V) // 8 - 1)
                    if 1 <= t <= STEPS:
                        u = t - 1
                        v.wait_ge(exped, i * STEPS + (u + 1))
                        if u >= NP:
                            v.wait_ge(normed, i * STEPS + (u - NP + 1))
                        nc.vector.reciprocal(ri[:, u % NP:u % NP + 1], rs[:, u % NP:u % NP + 1]).then_inc(inverse, 1)
                    if t < STEPS:
                        b, q, hh = step(t)
                        v.wait_ge(score_mm, i * STEPS + (t + 1))
                        nc.vector.reduce_max(mx[:, t % NP:t % NP + 1], ps_s[:, t % 2, 0:P * (q + 1)], AX.X).then_inc(maxed, 1)
                        v.wait_ge(maxed, i * STEPS + (t + 1))
                        nc.vector.tensor_scalar(nb[:, t % NP:t % NP + 1], mx[:, t % NP:t % NP + 1], -float(HD1) ** -0.5, None,
                                                ALU.mult).then_inc(shift, 1)
                    u = t - LAG_T
                    if 0 <= u < STEPS and u % 2 == 1:
                        move(nc.vector, v, i, u)
                    for n in range(NS):
                        if side[n][0] == t and side[n][1] == "wo" and t < STEPS + LAG_V:
                            add_wo(i, n)
                for n in range(NS - 2, NS):
                    add_wo(i, n)
            v.wait_ge(side_done, HP * NS + (PRE + 1))
            for c in range(NC):
                b = c * QB // L
                nc.vector.tensor_scalar(yT[:, QB * c:QB * (c + 1)], yT[:, QB * c:QB * (c + 1)], g.mod[:, 1, 2, b:b + 1], None,
                                        ALU.mult).then_inc(scaled, 1)
                v.wait_ge(turned_y, c + 1)
                xc = g.x[:, 4 * c:4 * c + 4, :].rearrange("p t d -> p (t d)")
                nc.vector.tensor_tensor(xc, xc, ps_e[:], ALU.add).then_inc(added, 1)
            v.wait_ge(added, NC)


def stage_route1(nc, g):
    with ExitStack() as ctx:
        def sb(n, s, dt=F32):
            return ctx.enter_context(nc.sbuf_tensor(n, s, dt))
        wr, db, iot = sb("wr", [P, E1]), sb("db", [E1, D]), sb("iot1", [P, E1])
        lg = sb("lg1", [P, NT, E1])
        top, idx, idf = sb("top", [P, NT, 8]), sb("idx", [P, NT, 8], U32), sb("idf", [P, NT, 8])
        col = sb("col1", [P, 6, NT])
        hot, wt = sb("hot", [P, 2, NT, E1]), sb("wt1", [P, NT, E1])
        wT = sb("wT", [E1, T])
        psl = ctx.enter_context(nc.psum_tensor("psl1", [P, NT, E1], F32))
        psw = ctx.enter_context(nc.psum_tensor("psw", [E1, 2, QB], F32))
        psy = ctx.enter_context(nc.psum_tensor("psy1", [P, 2, 4, D], F32))
        w_in, logits, chain, exped, weights, turned, moved, bias_mm, bias_done, maxes = sems(
            nc, g, "r1_w_in", "r1_logits", "r1_chain", "r1_exped", "r1_weights", "r1_turned", "r1_moved", "r1_bias_mm",
            "r1_bias_done", "r1_maxes")
        loads = [(wr[:], g.src["wr1"]), (db[:], g.src["db1"]), (iot[:], g.src["k_iota"][:, 0:E1])]
        block = ctx.enter_context(nc.Block())

        @block.sync
        def _(sp):
            for dst, src in loads:
                sp.dma_start(dst, src).then_inc(w_in, 16)

        @block.tensor
        def _(pe):
            pe.wait_ge(w_in, 16 * len(loads))
            for t in range(NT):
                last = nc.tensor.matmul(psl[:, t, :], g.hT[:, P * t:P * (t + 1)], wr[:], start=True, stop=True)
            last.then_inc(logits, 1)
            pe.wait_ge(weights, 1)
            for c in range(NC):
                if c >= 2:
                    pe.wait_ge(moved, c - 1)
                for k in range(4):
                    last = nc.tensor.transpose(psw[:, c % 2, P * k:P * (k + 1)], wt[:, 4 * c + k, :], g.ident[:])
                last.then_inc(turned, 1)
                pe.wait_ge(moved, c + 1)
                if c >= 2:
                    pe.wait_ge(bias_done, c - 1)
                for k in range(4):
                    last = nc.tensor.matmul(psy[:, c % 2, k, :], wT[:, QB * c + P * k:QB * c + P * (k + 1)], db[:],
                                            start=True, stop=True)
                last.then_inc(bias_mm, 1)

        @block.scalar
        def _(act):
            act.wait_ge(chain, 3)
            nc.scalar.activation(col[:, 1, :], col[:, 0, :], ACT.Exp).then_inc(exped, 1)
            for c in range(NC):
                act.wait_ge(turned, c + 1)
                nc.scalar.activation(wT[:, QB * c:QB * (c + 1)], psw[:, c % 2, :], ACT.Copy).then_inc(moved, 1)

        @block.vector
        def _(v):
            n = [0]

            def done(ins):
                n[0] += 1
                ins.then_inc(chain, 1)
                v.wait_ge(chain, n[0])

            def wide(c):
                return c.rearrange("p (t o) -> p t o", o=1).to_broadcast([P, NT, E1])

            iob = iot[:].rearrange("p (o e) -> p o e", o=1).to_broadcast([P, NT, E1])
            v.wait_ge(w_in, 16 * len(loads))
            v.wait_ge(logits, 1)
            done(nc.vector.tensor_copy(lg[:], psl[:]))
            for t in range(NT):
                nc.vector.max(top[:, t, :], lg[:, t, :]).then_inc(maxes, 1)
            for t in range(NT):
                v.wait_ge(maxes, t + 1)
                nc.vector.max_index(idx[:, t, :], top[:, t, :], lg[:, t, :]).then_inc(maxes, 1)
            v.wait_ge(maxes, 2 * NT)
            done(nc.vector.tensor_copy(idf[:], idx[:]))
            done(nc.vector.tensor_tensor(col[:, 0, :], top[:, :, 1], top[:, :, 0], ALU.subtract))
            v.wait_ge(exped, 1)
            done(nc.vector.tensor_scalar(col[:, 2, :], col[:, 1, :], 1.0, None, ALU.add))
            done(nc.vector.reciprocal(col[:, 3, :], col[:, 2, :]))
            done(nc.vector.tensor_tensor(col[:, 4, :], col[:, 1, :], col[:, 3, :], ALU.mult))
            for k in range(2):
                done(nc.vector.tensor_tensor(hot[:, k], iob, wide(idf[:, :, k]), ALU.is_equal))
                done(nc.vector.tensor_tensor(hot[:, k], hot[:, k], wide(col[:, 3 + k, :]), ALU.mult))
            nc.vector.tensor_tensor(wt[:], hot[:, 0], hot[:, 1], ALU.add).then_inc(weights, 1)
            v.wait_ge(weights, 1)
            nc.vector.tensor_scalar(g.wexp[:], wt[:].rearrange("p t e -> p e t"), 1.0 / GALPHA, None, ALU.mult).then_inc(weights, 1)
            for c in range(NC):
                v.wait_ge(bias_mm, c + 1)
                nc.vector.tensor_copy(g.y[:, 4 * c:4 * c + 4, :], psy[:, c % 2, :, :]).then_inc(bias_done, 1)
            v.wait_ge(weights, 2)
            v.wait_ge(bias_done, NC)


def stage_experts1(nc, g):
    with ExitStack() as ctx:
        def sb(n, s, dt=F32):
            return ctx.enter_context(nc.sbuf_tensor(n, s, dt))
        gu, dn, gb = sb("gu", [P, 2, 2, I1]), sb("dn", [P, 2, D]), sb("gub", [P, 2, 2])
        bu1 = sb("bu1", [P, 2])
        gt, sil, up, hid = sb("gt", [P, 2, QB]), sb("sil", [P, 2, QB]), sb("up", [P, 2, QB]), sb("hid1", [P, 2, QB])
        ps_g = ctx.enter_context(nc.psum_tensor("ps_g", [P, 2, QB], F32))
        ps_u = ctx.enter_context(nc.psum_tensor("ps_u", [P, 2, QB], F32))
        ps_d = ctx.enter_context(nc.psum_tensor("ps_d", [P, 2, 4, D], F32))
        gate_mm, up_mm, gate_cut, silu, up_cut, hid_done, down_mm, summed, bias1, scaled, added = sems(
            nc, g, "x_gate_mm", "x_up_mm", "x_gate_cut", "x_silu", "x_up_cut", "x_hid", "x_down_mm", "x_summed",
            "x_bias1", "x_scaled", "x_added")
        expert_in = two(nc, g, "x_expert_in")
        block = ctx.enter_context(nc.Block())
        C0 = 2
        BC = 2 * NC

        @block.sync
        def _(sp):
            with sp.Fori(0, E1 // 2) as i:
                for w in range(2):
                    sp.wait_ge(down_mm, i * BC + (NC * w + 1))
                    e = i * 2 + w
                    sp.dma_start(gu[:, w, :, :], g.src["gu1"][e]).then_inc(expert_in[w], 16)
                    sp.dma_start(dn[:, w, :], g.src["dn1"][e]).then_inc(expert_in[w], 16)
                    sp.dma_start(gb[:, w, :], g.src["gub1"][e]).then_inc(expert_in[w], 16)

        @block.tensor
        def _(pe):
            def down(i, k):
                w, s = k // NC % 2, k % 2
                pe.wait_ge(hid_done, i * BC + (k + 1))
                pe.wait_ge(summed, i * BC + (k + 1))
                for j in range(4):
                    last = nc.tensor.matmul(ps_d[:, s, j, :], hid[:, s, P * j:P * (j + 1)], dn[:, w, :], start=True, stop=True)
                last.then_inc(down_mm, 1)

            with pe.Fori(0, E1 // 2) as i:
                for k in range(BC):
                    w, c, s = k // NC, k % NC, k % 2
                    if c == 0:
                        pe.wait_ge(expert_in[w], i * 48 + 48)
                    hc = g.hT[:, QB * c:QB * (c + 1)]
                    if k >= 2:
                        pe.wait_ge(gate_cut, i * BC + (k - 1))
                    nc.tensor.matmul(ps_g[:, s, :], gu[:, w, 0, :], hc, start=True, stop=True).then_inc(gate_mm, 1)
                    if k >= 2:
                        pe.wait_ge(up_cut, i * BC + (k - 1))
                    nc.tensor.matmul(ps_u[:, s, :], gu[:, w, 1, :], hc, start=True, stop=True).then_inc(up_mm, 1)
                    if k >= 2:
                        down(i, k - 2)
                down(i, BC - 2)
                down(i, BC - 1)

        @block.scalar
        def _(act):
            with act.Fori(0, E1 // 2) as i:
                for k in range(BC):
                    act.wait_ge(gate_cut, i * BC + (k + 1))
                    if k >= 2:
                        act.wait_ge(hid_done, i * BC + (k - 1))
                    nc.scalar.activation(sil[:, k % 2, :], gt[:, k % 2, :], ACT.Silu, scale=GALPHA).then_inc(silu, 1)

        @block.vector
        def _(v):
            v.memset(gt[:, 0, 0:1], 0.0).then_inc(down_mm, NC)
            v.memset(gt[:, 0, 1:2], 0.0).then_inc(summed, C0)

            def cuts(i, k):
                w, s = k // NC, k % 2
                if k % NC == 0:
                    v.wait_ge(expert_in[w], i * 48 + 48)
                    nc.vector.tensor_scalar(bu1[:, w:w + 1], gb[:, w, 1:2], 1.0, None, ALU.add).then_inc(bias1, 1)
                    v.wait_ge(bias1, i * 2 + (w + 1))
                v.wait_ge(gate_mm, i * BC + (k + 1))
                if k >= 2:
                    v.wait_ge(silu, i * BC + (k - 1))
                nc.vector.tensor_scalar(gt[:, s, :], ps_g[:, s, :], gb[:, w, 0:1], GLIM, ALU.add, ALU.min).then_inc(gate_cut, 1)
                v.wait_ge(up_mm, i * BC + (k + 1))
                if k >= 2:
                    v.wait_ge(hid_done, i * BC + (k - 1))
                nc.vector.tensor_scalar(up[:, s, :], ps_u[:, s, :], bu1[:, w:w + 1], 1.0 - GLIM, ALU.add, ALU.max).then_inc(up_cut, 1)

            def hidden(i, k):
                s = k % 2
                v.wait_ge(silu, i * BC + (k + 1))
                v.wait_ge(up_cut, i * BC + (k + 1))
                v.wait_ge(down_mm, i * BC + (k - 1 + NC))
                nc.vector.scalar_tensor_tensor(out=hid[:, s, :], in0=up[:, s, :], scalar=1.0 + GLIM, in1=sil[:, s, :],
                                               op0=ALU.min, op1=ALU.mult).then_inc(hid_done, 1)

            def total(i, k):
                w, c, s = k // NC, k % NC, k % 2
                v.wait_ge(down_mm, i * BC + (k + 1 + NC))
                v.wait_ge(summed, i * BC + (k + C0 - 1))
                for j in range(4):
                    t = 4 * c + j
                    last = nc.vector.scalar_tensor_tensor(out=g.y[:, t, :], in0=ps_d[:, s, j, :],
                                                          scalar=g.wexp[:, bass.ds(i * 2 + w, 1), t],
                                                          in1=g.y[:, t, :], op0=ALU.mult, op1=ALU.add)
                last.then_inc(summed, 1)

            with v.Fori(0, E1 // 2) as i:
                for k in range(BC):
                    cuts(i, k)
                    if k >= 1:
                        hidden(i, k - 1)
                    if k >= 3:
                        total(i, k - 3)
                hidden(i, BC - 1)
                for k in range(BC - 3, BC):
                    total(i, k)
            v.wait_ge(summed, E1 * NC + C0)
            for b in range(B):
                yb, xb = g.y[:, TB * b:TB * (b + 1), :], g.x[:, TB * b:TB * (b + 1), :]
                nc.vector.tensor_tensor(yb, yb, g.bc[:, 5, b:b + 1, :].to_broadcast([P, TB, D]), ALU.mult).then_inc(scaled, 1)
                v.wait_ge(scaled, b + 1)
                nc.vector.tensor_tensor(xb, xb, yb, ALU.add).then_inc(added, 1)
            v.wait_ge(added, B)


def stage_store(nc, g):
    with ExitStack() as ctx:
        (out_done,) = sems(nc, g, "out_done")
        block = ctx.enter_context(nc.Block())

        @block.sync
        def _(sp):
            for b in range(B):
                sp.dma_start(g.out[L * b:L * (b + 1), :].rearrange("(t p) d -> p t d", p=P),
                             g.x[:, TB * b:TB * (b + 1), :]).then_inc(out_done, 16)
            sp.wait_ge(out_done, 16 * B)


def build(nc, a, out):
    g = Ctx(a)
    g.out = out
    with ExitStack() as ctx:
        def sb(n, s, dt=F32):
            return ctx.enter_context(nc.sbuf_tensor(n, s, dt))

        def dram(n, s, dt=F32):
            return nc.dram_tensor(n, s, dt, kind="Internal").ap()
        g.x = sb("x", [P, NT, D])
        g.ident, g.ones = sb("ident", [P, P]), sb("ones", [P, P])
        g.gamma, g.beta = sb("gamma", [P, 1]), sb("beta", [P, 1])
        g.mod = sb("mod", [P, 2, 6, B])
        g.bc = sb("bc", [P, 6, B, D])
        g.KS = dram("ks", [NBH, 6, HD0, L], BF16)
        g.QS = dram("qs", [NBH, 3, HD0, NF, L], BF16)
        g.PH = dram("phd", [NBH, NF, 4, L], BF16)
        g.NUM = dram("numd", [NBH + 1, 4, HD0 + 1, QB])
        stage_mod(nc, g)
        with ExitStack() as c0:
            g.v9 = c0.enter_context(nc.sbuf_tensor("v9", [P, NBH, TB, HD0 + 1], F32))
            g.alpha = c0.enter_context(nc.sbuf_tensor("alpha", [P, NBH * NF], F32))
            g.vsum = c0.enter_context(nc.sbuf_tensor("vsum", [P, B], F32))
            with ExitStack() as c1:
                g.h = c1.enter_context(nc.sbuf_tensor("h0", [P, NT, D], F32))
                g.hT = c1.enter_context(nc.sbuf_tensor("hT0", [P, T], F32))
                stage_norm(nc, g, 0, 0, False)
                g.vtok = g.h
                stage_qkv0(nc, g)
            stage_scores0(nc, g)
            stage_out0(nc, g)
        g.ROWS = dram("rowsd", [E0 * CAP + T, D])
        g.Y = dram("yd", [E0 * CAP, D])
        with ExitStack() as c0:
            g.gate = c0.enter_context(nc.sbuf_tensor("gate", [P, NT], F32))
            g.gidx = c0.enter_context(nc.sbuf_tensor("gidx", [P, NT], U32))
            g.sidx = c0.enter_context(nc.sbuf_tensor("sidx", [P, NT], U32))
            with ExitStack() as c1:
                g.h = c1.enter_context(nc.sbuf_tensor("h1", [P, NT, D], F32))
                g.hT = c1.enter_context(nc.sbuf_tensor("hT1", [P, T], F32))
                stage_norm(nc, g, 0, 3, True)
                stage_route0(nc, g)
            stage_experts0(nc, g)
            stage_combine0(nc, g)
            clear_sems(nc, g)
        with ExitStack() as c0:
            g.hT = c0.enter_context(nc.sbuf_tensor("hT2", [P, T], F32))
            with ExitStack() as c1:
                g.h = c1.enter_context(nc.sbuf_tensor("h2", [P, NT, D], F32))
                stage_norm(nc, g, 1, 0, False)
            stage_attention1(nc, g)
        with ExitStack() as c0:
            g.hT = c0.enter_context(nc.sbuf_tensor("hT3", [P, T], F32))
            g.h = c0.enter_context(nc.sbuf_tensor("h3", [P, NT, D], F32))
            stage_norm(nc, g, 1, 3, False)
            g.y = g.h
            g.wexp = c0.enter_context(nc.sbuf_tensor("wexp", [P, E1, NT], F32))
            stage_route1(nc, g)
            stage_experts1(nc, g)
        stage_store(nc, g)


def host_arrays(i):
    f = np.ascontiguousarray
    r = np.arange(P)
    sel = (r[None, :] // HD0 == np.arange(H0)[:, None]).astype(np.float32)
    bf16 = np.dtype("bfloat16")
    mrow = np.zeros((P, QB), bf16)
    mrow[SROWS - 1] = MAGIC
    col = lambda a: f(a.reshape(-1, 1))
    wqkv = f(np.stack([i["L1_attn_" + n].reshape(HP, P, D).transpose(0, 2, 1) for n in ("wq", "wk", "wv")], axis=2))
    return {
        "x_d": f(i["L0_attn_x"].reshape(T, D)),
        "c0": f(i["L0_c"].T), "c1": f(i["L1_c"].T), "wm0": i["L0_wmod"], "wm1": i["L1_wmod"],
        "gamma_d": col(i["L0_attn_gamma"]), "beta_d": col(i["L0_attn_beta"]),
        "wq0": f(i["L0_attn_Wq"].T), "wk0": f(i["L0_attn_Wk"].T), "wv0": f(i["L0_attn_Wv"].T), "wo0": f(i["L0_attn_Wo"].T),
        "bq0": col(i["L0_attn_bq"]), "bk0": col(i["L0_attn_bk"]),
        "bv0": f(i["L0_attn_bv"].reshape(1, D)), "bo0": f(i["L0_attn_bo"].reshape(1, D)),
        "temp": f(i["L0_attn_temperature"].reshape(1, 1)), "phi": col(i["L0_attn_phi"]),
        "alpha_d": f(np.tile(i["L0_attn_alpha"].reshape(1, -1), (1, B))),
        "wg0": i["L0_ffn_Wg"], "bg0": f(i["L0_ffn_bg"].reshape(1, E0)), "w1": i["L0_ffn_W1"],
        "b1": f(i["L0_ffn_b1"].reshape(E0, HF // P, P).transpose(2, 0, 1)),
        "w2": f(i["L0_ffn_W2"].reshape(E0, HF // P, P, D).transpose(0, 2, 1, 3)), "b2": f(i["L0_ffn_b2"].reshape(E0, 1, D)),
        "wqkv1": np.concatenate([wqkv, wqkv[:1]]), "wo1": f(i["L1_attn_wo"].T.reshape(HP, P, D)),
        "wr1": i["L1_ffn_router_weight"], "db1": i["L1_ffn_down_proj_bias"], "dn1": i["L1_ffn_down_proj"],
        "gu1": f(i["L1_ffn_gate_up_proj"].reshape(E1, D, I1, 2).transpose(0, 1, 3, 2)),
        "gub1": f(i["L1_ffn_gate_up_proj_bias"].reshape(E1, I1, 2)),
        "k_iota": np.tile(np.arange(E0, dtype=np.float32), (P, 1)),
        "k_tok": (E0 * CAP + np.arange(NT)[None, :] * P + r[:, None]).astype(np.float32),
        "k_tri": (r[:, None] < r[None, :]).astype(bf16), "k_one": np.ones((P, P), bf16),
        "k_identb": np.eye(P).astype(bf16),
        "k_mask": np.where(r[None, :] > r[:, None], NEG, 0.0).astype(bf16),
        "k_ident": np.eye(P, dtype=np.float32), "k_sel": sel, "k_mrow": mrow,
    }


def kernel(**inputs):
    import concourse.bacc as bacc
    from concourse.bass_utils import run_bass_kernel_spmd

    nc = bacc.Bacc("TRN2", target_bir_lowering=False, num_devices=1)
    arrays = host_arrays({k: np.asarray(v) for k, v in inputs.items()})
    aps = {k: nc.dram_tensor("in_" + k, a.shape, mybir.dt.from_np(a.dtype), kind="ExternalInput").ap() for k, a in arrays.items()}
    out = nc.dram_tensor("out_x", (T, D), F32, kind="ExternalOutput").ap()
    build(nc, aps, out)
    got = run_bass_kernel_spmd(nc, [{"in_" + k: a for k, a in arrays.items()}], core_ids=[0])
    return got.results[0]["out_x"].reshape(B, L, D)
```
